# Optimizing a Trainium2 kernel written in Bass

```python
import numpy as np
import jax
import jax.numpy as jnp

def _softmax(x, axis=-1):
    return jax.nn.softmax(x, axis=axis)

def _gelu(x):
    return jax.nn.gelu(x, approximate=True)

def _silu(x):
    return jax.nn.silu(x)

def _sigmoid(x):
    return jax.nn.sigmoid(x)

def _layernorm(x, axis=-1, eps=1e-05):
    m = jnp.mean(x, axis=axis, keepdims=True)
    v = jnp.var(x, axis=axis, keepdims=True)
    return (x - m) / jnp.sqrt(v + eps)

def _scatter_add(tgt, idx, src, axis=0):
    return tgt.at[idx].add(src)

def _segment_sum(src, seg, n):
    return jax.ops.segment_sum(src, seg, n)
kernel_name = 'mk_gnn_resnorm_d1_gnn_r64_adf00f'

def setup_inputs(seed: int=0):
    np.random.seed(seed)
    _w = jnp.asarray

    def _rec_inputs():
        import jax
        import jax.numpy as jnp
        _gk = jax.random.key(seed)
        x = -0.0001006 + 1 * jax.random.normal(jax.random.fold_in(_gk, 1), (100000, 96), jnp.float32)
        src = jax.random.randint(jax.random.fold_in(_gk, 2), (50000,), 0, 100000, jnp.int32)
        dst = jnp.minimum((100000 * jax.random.uniform(jax.random.fold_in(_gk, 3), (50000,)) ** 2.0).astype(jnp.int32), 99999)
        _o = jnp.argsort(dst, stable=True)
        src = src[_o]
        dst = dst[_o]
        edge_attr_32 = 0.000196303 + 1.00016 * jax.random.normal(jax.random.fold_in(_gk, 11), (50000, 32), jnp.float32)
        return (x, src, dst, edge_attr_32)
    x, src, dst, edge_attr_32 = _rec_inputs()

    def _L0_gnn_setup():
        import jax, jax.numpy as jnp
        import numpy as np
        N, E = (50000, 12500)
        DIN = DOUT = 96
        DE = 32

        def _egnn_conv(x, src, dst, edge_attr, W_msg, W_edge, W_root, b):
            msg = x[src] @ W_msg + edge_attr @ W_edge
            agg = jax.ops.segment_max(msg, dst, num_segments=x.shape[0])
            agg = jnp.where(jnp.isneginf(agg), 0.0, agg)
            return agg + x @ W_root + b
        key = jax.random.key(seed)
        ks = jax.random.split(key, 10)
        rn = lambda k, sh, sc: jax.random.normal(k, sh, jnp.float32) * sc
        return {'X': rn(ks[0], (N, DIN), 1.0), 'edge_index': jax.random.randint(ks[1], (2, E), 0, N, jnp.int32), 'edge_attr': rn(ks[2], (E, DE), 1.0), 'W1_msg': rn(ks[3], (DIN, DOUT), DIN ** (-0.5)), 'W1_edge': rn(ks[4], (DE, DOUT), DE ** (-0.5)), 'W1_root': rn(ks[5], (DIN, DOUT), DIN ** (-0.5)), 'b1': jnp.zeros((DOUT,), jnp.float32), 'W2_msg': rn(ks[6], (DOUT, DOUT), DOUT ** (-0.5)), 'W2_edge': rn(ks[7], (DE, DOUT), DE ** (-0.5)), 'W2_root': rn(ks[8], (DOUT, DOUT), DOUT ** (-0.5)), 'b2': jnp.zeros((DOUT,), jnp.float32)}
    _L0_gnn_all = _L0_gnn_setup()
    _L0_gnn_in = {k: v for k, v in _L0_gnn_all.items() if k in ('W1_msg', 'W1_edge', 'W1_root', 'b1', 'W2_msg', 'W2_edge', 'W2_root', 'b2')}
    del _L0_gnn_all
    return {'x': x, 'src': src, 'dst': dst, 'edge_attr_32': edge_attr_32, 'L0_gnn_W1_msg': _L0_gnn_in['W1_msg'], 'L0_gnn_W1_edge': _L0_gnn_in['W1_edge'], 'L0_gnn_W1_root': _L0_gnn_in['W1_root'], 'L0_gnn_b1': _L0_gnn_in['b1'], 'L0_gnn_W2_msg': _L0_gnn_in['W2_msg'], 'L0_gnn_W2_edge': _L0_gnn_in['W2_edge'], 'L0_gnn_W2_root': _L0_gnn_in['W2_root'], 'L0_gnn_b2': _L0_gnn_in['b2']}

def reference(x, src, dst, edge_attr_32, L0_gnn_W1_msg, L0_gnn_W1_edge, L0_gnn_W1_root, L0_gnn_b1, L0_gnn_W2_msg, L0_gnn_W2_edge, L0_gnn_W2_root, L0_gnn_b2):
    import jax
    import jax.numpy as jnp

    def _L0_gnn_ref(X, edge_index, edge_attr, W1_msg, W1_edge, W1_root, b1, W2_msg, W2_edge, W2_root, b2):
        import jax, jax.numpy as jnp
        import numpy as np
        N, E = (50000, 12500)
        DIN = DOUT = 96
        DE = 32

        def _egnn_conv(x, src, dst, edge_attr, W_msg, W_edge, W_root, b):
            msg = x[src] @ W_msg + edge_attr @ W_edge
            agg = jax.ops.segment_max(msg, dst, num_segments=x.shape[0])
            agg = jnp.where(jnp.isneginf(agg), 0.0, agg)
            return agg + x @ W_root + b
        src, dst = (edge_index[0], edge_index[1])
        c1 = jax.nn.leaky_relu(_egnn_conv(X, src, dst, edge_attr, W1_msg, W1_edge, W1_root, b1))
        c2 = jax.nn.leaky_relu(_egnn_conv(c1, src, dst, edge_attr, W2_msg, W2_edge, W2_root, b2))
        return c2
    edge_index = jnp.stack([src, dst])
    x = _layernorm(x + _L0_gnn_ref(x, edge_index, edge_attr_32, L0_gnn_W1_msg, L0_gnn_W1_edge, L0_gnn_W1_root, L0_gnn_b1, L0_gnn_W2_msg, L0_gnn_W2_edge, L0_gnn_W2_root, L0_gnn_b2), axis=-1)
    return x

_drawn_inputs = setup_inputs


def setup_inputs(seed=0):
    import zlib

    import numpy as np

    out = dict(_drawn_inputs(seed))
    spreads = {'L0_gnn_b1': (0.0, 0.1), 'L0_gnn_b2': (0.0, 0.1)}
    factors = {}
    for name, (base, spread) in spreads.items():
        noise = np.random.default_rng([zlib.crc32(name.encode()), seed]).standard_normal(out[name].shape)
        drawn = base * np.exp(spread * noise) if base else spread * noise
        out[name] = jnp.asarray(drawn.astype(out[name].dtype))
    for name, factor in factors.items():
        out[name] = (out[name] * factor).astype(out[name].dtype)
    return out
```

```python
from contextlib import ExitStack

import concourse.bass as bass
from concourse import mybir

F32 = mybir.dt.float32
BF16 = mybir.dt.bfloat16
I32 = mybir.dt.int32
ALU = mybir.AluOpType
ACT = mybir.ActivationFunctionType
AX_X = mybir.AxisListType.X

P = 128
GROUP = 4
RI = 16
SB = P * RI
SPARE = 2 * SB
SLOPE = 0.01
EPS = 1e-5
BIG = 3.3895313892515355e38
DMA = 16
NB_OUT = 3
ACT_TILES = 6
META_STEPS = 21
NORM_STEPS = 6
SCAN = GROUP * P


def gnn(nc, x, src, dst, edge_attr, weights, out):
    N, D = x.shape
    E, DE = edge_attr.shape
    K = D + DE
    NSB, E_LEFT = divmod(E, SB)
    NBL, N_LEFT = divmod(N, SB)
    EJ = 8
    EP, NP = E_LEFT // EJ, N_LEFT // RI
    assert K == P and EP * EJ == E_LEFT and NP * RI == N_LEFT and EP <= P and NP <= P
    assert NSB % 2 == 0 and NBL == 2 * NSB and NBL % NB_OUT == 0
    HALF = RI // 2
    NG = RI // GROUP
    EG_LEFT = EJ // GROUP
    SB_USES = (NSB // 2 + 1, NSB // 2)
    EDGE_GROUPS = NSB * NG + EG_LEFT
    BLOCKS = NBL + 1
    MP = 125
    MC = E // MP
    assert MP * MC == E

    with ExitStack() as ctx:
        def sb(name, shape, dt):
            return ctx.enter_context(nc.sbuf_tensor(name, shape, dt))

        def psum(name, shape):
            return ctx.enter_context(nc.psum_tensor(name, shape, F32))

        def sem(name):
            return ctx.enter_context(nc.semaphore(name))

        def sems(name, n=2):
            return [sem(f"{name}{i}") for i in range(n)]

        root = [nc.dram_tensor(f"root{i}", (N + SPARE, D), F32, kind="Internal").ap() for i in range(2)]
        rows_to_dram = nc.dram_tensor("scatter_rows", (E,), I32, kind="Internal").ap()
        keep_dram = nc.dram_tensor("keep_row", (E,), BF16, kind="Internal").ap()
        needs_dram = nc.dram_tensor("needs_table", (BLOCKS, 2), I32, kind="Internal").ap()

        hold = sb("hold", [P, NSB * RI + EJ, D], F32)
        shared = sb("shared", [P, 6 * RI * D], F32)
        nodes_in = sb("nodes_in", [P, 2, RI * D], F32)
        root_out = sb("root_out", [P, 2, HALF * D], F32)
        nodes_t = sb("nodes_t", [P, 2, GROUP * P], F32)
        edges_t = sb("edges_t", [P, GROUP * P], F32)
        attr = sb("attr", [P, RI * DE], F32)
        ident = sb("ident", [P, P], F32)
        w_root = sb("w_root", [P, 2, D], F32)
        w_edge = sb("w_edge", [P, 2, D], F32)
        src_all = sb("src_all", [P, (NSB + 2) * RI], I32)
        src_now = sb("src_now", [P, 2, RI], I32)
        rows_now = sb("rows_now", [P, 2, RI], I32)
        stats = sb("stats", [P, RI, 6], F32)
        small = sb("small", [P, 6, RI], F32)
        slopes = sb("slopes", [P, 1], F32)
        eps = sb("eps", [P, 1], F32)
        first = sb("first", [P, NSB + 1], I32)
        below = sb("below", [P, 2, NSB + 1], F32)
        share = sb("share", [P, 2, NSB + 1], F32)
        bound_i = sb("bound_i", [P, 1], I32)
        bound = sb("bound", [P, 1], F32)
        needs = sb("needs", [P, 2], I32)
        needs_f = sb("needs_f", [P, 2], F32)

        gathered = [shared[:, i * RI * K:(i + 1) * RI * K].rearrange("p (r k) -> p r k", k=K) for i in range(2)]
        msgs = [shared[:, (2 + i) * SB:(3 + i) * SB] for i in range(2)]
        keep = shared[:, 4 * SB:4 * SB + SB // 2].bitcast(BF16)
        last_root = [shared[:, i * RI * D:(i + 1) * RI * D] for i in range(NB_OUT)]
        last_x = [shared[:, (NB_OUT + i) * RI * D:(NB_OUT + i + 1) * RI * D] for i in range(NB_OUT)]

        flat = hold[:].rearrange("p t d -> p (t d)")
        meta_at = (NSB * RI + EJ) * D

        def meta(i, dt):
            a = flat[0:MP, meta_at - (i + 1) * MC:meta_at - i * MC]
            return a if dt is F32 else a.bitcast(dt)

        this_dst, next_dst, prev_dst, number = (meta(i, I32) for i in range(4))
        same_next, same_prev, spare, step = (meta(4 + i, F32) for i in range(4))
        target = meta(8, I32)
        keep_all = flat[0:MP, meta_at - 9 * MC - MC // 2:meta_at - 9 * MC].bitcast(BF16)
        zero_rows = flat[:, 0:RI * D]

        nt_ps = [psum(f"nt_ps{i}", [P, GROUP * P]) for i in range(2)]
        no_ps = [psum(f"no_ps{i}", [P, GROUP * P]) for i in range(2)]
        et_ps = [psum(f"et_ps{i}", [P, GROUP * P]) for i in range(2)]
        em_ps = psum("em_ps", [P, GROUP * P])
        eb_ps = psum("eb_ps", [P, GROUP * P])

        zeroed, ident_done, weights_in, src_in = sem("zeroed"), sem("ident_done"), sem("weights_in"), sem("src_in")
        preset, dst_in, meta_step, meta_out = sem("preset"), sem("dst_in"), sem("meta_step"), sem("meta_out")
        numbered, spare_zeroed = sem("numbered"), sem("spare_zeroed")
        block_in, block_turned = sems("block_in"), sems("block_turned")
        nt_full, nt_free, nt_scaled = sems("nt_full", NG - 1), sems("nt_free"), sems("nt_scaled")
        no_full, no_free = sems("no_full"), sems("no_free")
        root_stored = sems("root_stored")
        src_staged, rows_in, edges_turned = sems("src_staged"), sems("rows_in"), sems("edges_turned")
        attr_in, attr_placed = sem("attr_in"), sem("attr_placed")
        et_full, et_free, et_scaled = sems("et_full", NG - 1), sems("et_free"), sems("et_scaled")
        em_full, em_free = sem("em_full"), sem("em_free")
        keep_in, scan_part, scanned = sem("keep_in"), sem("scan_part"), sem("scanned")
        eb_full, eb_free = sem("eb_full"), sem("eb_free")
        pool_open = sem("pool_open")
        staged, scattered = sems("staged"), [sems("scattered_a"), sems("scattered_b")]
        last_in = sems("last_in", NB_OUT)
        summed, spread = sem("summed"), sem("spread")
        vec_step, scaled, vec_normed = sem("vec_step"), sem("scaled"), sem("vec_normed")
        act_normed, out_stored = sem("act_normed"), sems("out_stored", NB_OUT)

        def blocks(a, width):
            return a[0:NBL * SB, :].rearrange("(b p r) d -> b p (r d)", p=P, r=width)

        def rows_left(a):
            return a[NBL * SB:N, :].rearrange("(p r) d -> p (r d)", r=RI)

        h_of = [x, root[0]]
        src_full = src[0:NSB * SB].rearrange("(s p r) -> p s r", p=P, r=RI)
        src_left = src[NSB * SB:E].rearrange("(p r) -> p r", r=EJ)
        to_full = rows_to_dram[0:NSB * SB].rearrange("(s p r) -> s p r", p=P, r=RI)
        to_left = rows_to_dram[NSB * SB:E].rearrange("(p r) -> p r", r=EJ)
        attr_full = edge_attr[0:NSB * SB, :].rearrange("(s p r) d -> s p (r d)", p=P, r=RI)
        attr_left = edge_attr[NSB * SB:E, :].rearrange("(p r) d -> p (r d)", r=EJ)
        keep_full = keep_dram[0:NSB * SB].rearrange("(s a e) -> s a e", s=NSB, a=1)
        keep_left = keep_dram[NSB * SB:E].rearrange("(a e) -> a e", a=1)
        dst_row = dst.rearrange("(a e) -> a e", a=1)

        LAYER_ROWS = ((NSB // 2 * RI + EJ) * DMA, NSB // 2 * RI * DMA)

        class Slot:

            def __init__(self, layer, it, odd):
                self.layer, self.odd, self.full = layer, odd, it is not None
                self.s = 2 * it + odd if self.full else NSB
                self.half = it if self.full else NSB // 2
                self.use = layer * SB_USES[odd] + self.half
                self.order = layer * (NSB + 1) + self.s
                self.ep, self.ej = (P, RI) if self.full else (EP, EJ)
                self.egroups = NG if self.full else EG_LEFT
                self.cols = self.ep * self.ej
                self.np = P if self.full else NP
                self.nblocks = 2 if self.full else 1
                self.ngroups = NG * self.nblocks

            def block(self, k):
                return 2 * self.s + k

            def block_use(self, k):
                return self.layer * (NSB + (1 if k == 0 else 0)) + self.s

            def ngroup_use(self, j):
                return self.layer * BLOCKS * (NG // 2) + self.block(j // NG) * (NG // 2) + (j % NG) // 2

            def root_use(self, j):
                return self.layer * BLOCKS + self.block(j // NG)

            def egroup_use(self, q):
                return self.layer * (EDGE_GROUPS // 2) + self.s * (NG // 2) + q // 2

            def egroup(self, q):
                return self.layer * EDGE_GROUPS + self.s * NG + q

            def rows(self):
                return self.layer * LAYER_ROWS[self.odd] + (self.half * RI + self.ej) * DMA

            def nodes_turned(self, j):
                if j % NG == NG - 1:
                    return block_turned[j // NG], self.block_use(j // NG) + 1
                return nt_full[j % NG], self.root_use(j) + 1

            def edges_turned(self, q):
                if q == self.egroups - 1:
                    return edges_turned[self.odd], self.use + 1
                return et_full[q], (self.order if q == 0 else self.layer * NSB + self.s) + 1

            def scan_parts(self):
                return self.layer * (NSB * (NG - 1) + EG_LEFT - 1) + self.s * (NG - 1)

        def slots(eng, layer, body):
            for odd in range(2):
                body(Slot(layer, 0, odd))
            with eng.Fori(1, NSB // 2) as it:
                for odd in range(2):
                    body(Slot(layer, it, odd))
            body(Slot(layer, None, 0))

        def root_to_sbuf(eng, t, j):
            bank, half = j % 2, (j % NG) // 2
            eng.wait_ge(no_full[bank], t.ngroup_use(j) + 1)
            if j % 2 == 0:
                eng.wait_ge(root_stored[half], DMA * t.root_use(j))
            at = slice((j % 2) * GROUP * D, (j % 2 + 1) * GROUP * D)
            to, of = root_out[0:t.np, half, at], no_ps[bank][0:t.np, 0:GROUP * D]
            return lambda copy: copy(to, of).then_inc(no_free[bank], 1)

        block = ctx.enter_context(nc.Block())

        @block.sync
        def _(sp):
            sp.dma_start(src_all[:, 0:NSB * RI].rearrange("p (s r) -> p s r", r=RI), src_full).then_inc(src_in, DMA)
            sp.wait_ge(preset, 1)
            sp.dma_start(src_all[0:EP, NSB * RI:NSB * RI + EJ], src_left).then_inc(src_in, DMA)
            for layer in range(2):
                w_msg, w_e, w_r, bias = weights[4 * layer:4 * layer + 4]
                sp.dma_start(w_edge[0:D, layer, :], w_msg).then_inc(weights_in, DMA)
                sp.dma_start(w_edge[D:K, layer, :], w_e).then_inc(weights_in, DMA)
                sp.dma_start(w_root[0:D, layer, :], w_r).then_inc(weights_in, DMA)
                sp.dma_start(w_root[D:D + 1, layer, :], bias.rearrange("(a d) -> a d", a=1)).then_inc(weights_in, DMA)
            sp.dma_start(this_dst, dst.rearrange("(p c) -> p c", c=MC)).then_inc(dst_in, DMA)
            sp.wait_ge(preset, 3)
            last = (MP - 1) * MC
            sp.dma_start(next_dst[0:MP - 1, :], dst[1:last + 1].rearrange("(p c) -> p c", c=MC)).then_inc(dst_in, DMA)
            sp.dma_start(next_dst[MP - 1:MP, 0:MC - 1], dst_row[:, last + 1:E]).then_inc(dst_in, DMA)
            sp.dma_start(prev_dst[0:1, 1:MC], dst_row[:, 0:MC - 1]).then_inc(dst_in, DMA)
            sp.dma_start(prev_dst[1:MP, :], dst[MC - 1:E - 1].rearrange("(p c) -> p c", c=MC)).then_inc(dst_in, DMA)
            with nc.allow_non_contiguous_dma(reason="the first dst of each superblock"):
                sp.dma_start(first[0:BLOCKS, :], dst_row[:, 0:E:SB].to_broadcast([BLOCKS, NSB + 1])).then_inc(dst_in, DMA)
            sp.wait_ge(zeroed, 1)
            for layer in range(2):
                for i in range(SPARE // SB):
                    to = root[layer][N + i * SB:N + (i + 1) * SB, :].rearrange("(p r) d -> p (r d)", r=RI)
                    sp.dma_start(to, zero_rows).then_inc(spare_zeroed, DMA)
            sp.wait_ge(meta_step, META_STEPS)
            sp.dma_start(rows_to_dram.rearrange("(p c) -> p c", c=MC), target).then_inc(meta_out, DMA)
            sp.dma_start(keep_dram.rearrange("(p c) -> p c", c=MC), keep_all).then_inc(meta_out, DMA)
            sp.dma_start(needs_dram, needs[0:BLOCKS, :]).then_inc(meta_out, DMA)
            sp.wait_ge(meta_out, 3 * DMA)

            def loads(t):
                h = h_of[t.layer]
                for k in range(t.nblocks):
                    sp.wait_ge(block_turned[k], t.block_use(k))
                    if t.full:
                        sp.dma_start(nodes_in[:, k, :], blocks(h, RI)[t.block(k)]).then_inc(block_in[k], DMA)
                    else:
                        sp.dma_start(nodes_in[0:NP, k, :], rows_left(h)).then_inc(block_in[k], DMA)
                    if k == 0:
                        sp.wait_ge(attr_placed, t.order)
                        if t.full:
                            sp.dma_start(attr[:], attr_full[t.s]).then_inc(attr_in, DMA)
                        else:
                            sp.dma_start(attr[0:EP, 0:EJ * DE], attr_left).then_inc(attr_in, DMA)
                sp.wait_ge(scanned, t.order)
                view = keep_full[t.s] if t.full else keep_left
                sp.dma_start(keep[0:D, 0:t.cols], view.to_broadcast([D, t.cols])).then_inc(keep_in, DMA)

            def stage(t):
                sp.wait_ge(scattered[t.layer][t.odd], t.half * RI * DMA)
                if t.full:
                    rows = hold[:, bass.ds(t.s * RI, RI), :].rearrange("p r d -> p (r d)")
                    sp.dma_start(nodes_in[:, t.odd, :], rows).then_inc(staged[t.odd], DMA)
                    sp.dma_start(rows_now[:, t.odd, :], to_full[t.s]).then_inc(staged[t.odd], DMA)
                else:
                    rows = hold[0:EP, NSB * RI:, :].rearrange("p r d -> p (r d)")
                    sp.dma_start(nodes_in[0:EP, t.odd, 0:EJ * D], rows).then_inc(staged[t.odd], DMA)
                    sp.dma_start(rows_now[0:EP, t.odd, 0:EJ], to_left).then_inc(staged[t.odd], DMA)

            for layer in range(2):
                slots(sp, layer, loads)
                sp.wait_ge(eb_free, (layer + 1) * EDGE_GROUPS)
                sp.wait_ge(block_turned[0], (layer + 1) * (NSB + 1))
                sp.wait_ge(block_turned[1], (layer + 1) * NSB)
                slots(sp, layer, stage)
                if layer == 0:
                    for odd in range(2):
                        sp.wait_ge(scattered[0][odd], LAYER_ROWS[odd])

        @block.gpsimd
        def _(pool):
            nc.gpsimd.memset(ident[:], 0.0).then_inc(numbered, 1)
            pool.wait_ge(numbered, 1)
            nc.gpsimd.affine_select(out=ident[:], in_=ident[:], compare_op=ALU.not_equal, fill=1.0, base=0,
                                    pattern=[[-1, P]], channel_multiplier=1).then_inc(ident_done, 1)
            nc.gpsimd.iota(number, pattern=[[1, MC]], base=0, channel_multiplier=MC).then_inc(numbered, 1)
            nc.gpsimd.iota(bound_i[:], pattern=[[0, 1]], base=SB, channel_multiplier=SB).then_inc(numbered, 1)

            def gather(t):
                pool.wait_ge(src_staged[t.odd], t.layer * SB_USES[0] + t.half + 1)
                pool.wait_ge(edges_turned[t.odd], t.use)
                pool.sem_inc(pool_open, 1)
                for i in range(t.ej):
                    nc.gpsimd.indirect_dma_start(
                        out=gathered[t.odd][0:t.ep, i, 0:D], out_offset=None, in_=h_of[t.layer],
                        in_offset=bass.IndirectOffsetOnAxis(ap=src_now[0:t.ep, t.odd, i:i + 1], axis=0),
                    ).then_inc(rows_in[t.odd], DMA)

            def scatter(t):
                pool.wait_ge(staged[t.odd], 2 * DMA * (t.use + 1))
                pool.sem_inc(pool_open, 1)
                for i in range(t.ej):
                    nc.gpsimd.indirect_dma_start(
                        out=root[t.layer],
                        out_offset=bass.IndirectOffsetOnAxis(ap=rows_now[0:t.ep, t.odd, i:i + 1], axis=0),
                        in_=nodes_in[0:t.ep, t.odd, i * D:(i + 1) * D], in_offset=None, compute_op=ALU.add,
                    ).then_inc(scattered[t.layer][t.odd], DMA)

            for layer in range(2):
                slots(pool, layer, gather)
                pool.wait_ge(spare_zeroed, 2 * (SPARE // SB) * DMA)
                for half in range(2):
                    pool.wait_ge(root_stored[half], (layer + 1) * BLOCKS * DMA)
                slots(pool, layer, scatter)
                for odd in range(2):
                    pool.wait_ge(scattered[layer][odd], LAYER_ROWS[odd])

        @block.tensor
        def _(pe):
            pe.wait_ge(ident_done, 1)
            pe.wait_ge(weights_in, 8 * DMA)
            pe.wait_ge(zeroed, 2)

            def turn_nodes(t, j):
                k, g, bank = j // NG, j % NG, j % 2
                if g == 0:
                    pe.wait_ge(block_in[k], DMA * (t.block_use(k) + 1))
                pe.wait_ge(nt_free[bank], t.ngroup_use(j))
                for i in range(GROUP):
                    at = (g * GROUP + i) * D
                    last = nc.tensor.transpose(nt_ps[bank][0:D, i * t.np:(i + 1) * t.np],
                                               nodes_in[0:t.np, k, at:at + D], ident[0:t.np, 0:t.np])
                last.then_inc(t.nodes_turned(j)[0], 1)

            def root_of(t, j):
                bank = j % 2
                pe.wait_ge(nt_free[bank], t.ngroup_use(j) + 1)
                pe.wait_ge(no_free[bank], t.ngroup_use(j))
                for i in range(GROUP):
                    last = nc.tensor.matmul(no_ps[bank][0:t.np, i * D:(i + 1) * D],
                                            nodes_t[0:D + 1, bank, i * t.np:(i + 1) * t.np],
                                            w_root[0:D + 1, t.layer, :], start=True, stop=True)
                last.then_inc(no_full[bank], 1)

            def turn_edges(t, q):
                bank = q % 2
                if q == 0:
                    pe.wait_ge(rows_in[t.odd], t.rows())
                    pe.wait_ge(attr_placed, t.order + 1)
                pe.wait_ge(et_free[bank], t.egroup_use(q))
                for i in range(GROUP):
                    last = nc.tensor.transpose(et_ps[bank][:, i * t.ep:(i + 1) * t.ep],
                                               gathered[t.odd][0:t.ep, q * GROUP + i, :], ident[0:t.ep, 0:t.ep])
                last.then_inc(t.edges_turned(q)[0], 1)

            def messages(t, q):
                bank = q % 2
                pe.wait_ge(et_free[bank], t.egroup_use(q) + 1)
                pe.wait_ge(em_free, t.egroup(q))
                ins = nc.tensor.matmul(em_ps[0:D, 0:GROUP * t.ep], w_edge[:, t.layer, :],
                                       edges_t[:, 0:GROUP * t.ep], start=True, stop=True)
                ins.then_inc(em_full, 1)

            def turn_back(t, q):
                pe.wait_ge(scanned, t.order + 1)
                pe.wait_ge(eb_free, t.egroup(q))
                for i in range(GROUP):
                    cols = msgs[t.odd][0:D, q * GROUP + i:t.cols:t.ej]
                    last = nc.tensor.transpose(eb_ps[0:t.ep, i * D:(i + 1) * D], cols, ident[0:D, 0:D])
                last.then_inc(eb_full, 1)

            def slot(t):
                for j in range(t.ngroups + 1):
                    if j < t.ngroups:
                        turn_nodes(t, j)
                    if j < t.egroups:
                        turn_edges(t, j)
                    if j >= 1:
                        root_of(t, j - 1)
                    if 1 <= j <= t.egroups:
                        messages(t, j - 1)
                for q in range(t.egroups):
                    turn_back(t, q)

            for layer in range(2):
                slots(pe, layer, slot)

        @block.scalar
        def _(act):
            def read_nodes(t, j):
                bank = j % 2
                act.wait_ge(*t.nodes_turned(j))
                act.wait_ge(no_full[bank], t.ngroup_use(j))
                cols = slice(0, GROUP * t.np)
                nc.scalar.activation(nodes_t[0:D, bank, cols], nt_ps[bank][0:D, cols], ACT.Copy,
                                     scale=SLOPE if t.layer else 1.0,
                                     ).then_inc((nt_scaled if t.layer else nt_free)[bank], 1)

            def read_edges(t, q):
                bank = q % 2
                act.wait_ge(*t.edges_turned(q))
                act.wait_ge(em_full, t.egroup(q))
                cols = slice(0, GROUP * t.ep)
                nc.scalar.activation(edges_t[:, cols], et_ps[bank][:, cols], ACT.Copy,
                                     scale=slopes[:, 0:1] if t.layer else 1.0,
                                     ).then_inc((et_scaled if t.layer else et_free)[bank], 1)

            def read_messages(t, q):
                act.wait_ge(em_full, t.egroup(q) + 1)
                if q == 0:
                    act.wait_ge(scanned, t.order)
                to = msgs[t.odd][0:D, 0:t.cols].rearrange("d (p r) -> d p r", r=t.ej)[:, :, q * GROUP:(q + 1) * GROUP]
                nc.scalar.activation(to, em_ps[0:D, 0:GROUP * t.ep].rearrange("d (i p) -> d p i", i=GROUP),
                                     ACT.Copy).then_inc(em_free, 1)

            def read_root(t, j):
                root_to_sbuf(act, t, j)(nc.scalar.copy)

            def store_root(t, j):
                half = (j % NG) // 2
                act.wait_ge(no_free[0], t.ngroup_use(j - 1) + 1)
                act.wait_ge(no_free[1], t.ngroup_use(j) + 1)
                view = root[t.layer]
                at = slice(half * HALF * D, (half + 1) * HALF * D)
                if t.full:
                    to = blocks(view, RI)[t.block(j // NG)][:, at]
                else:
                    to = rows_left(view)[:, at]
                act.dma_start(to, root_out[0:t.np, half, :]).then_inc(root_stored[half], DMA)

            def slot(t):
                for j in range(t.ngroups + 1):
                    if j < t.ngroups:
                        read_nodes(t, j)
                    if j < t.egroups:
                        read_edges(t, j)
                    if 1 <= j <= t.egroups:
                        read_messages(t, j - 1)
                    if t.layer and j >= 1:
                        read_root(t, j - 1)
                    if j >= 3 and j % 2:
                        store_root(t, j - 2)
                store_root(t, t.ngroups - 1)

            for layer in range(2):
                slots(act, layer, slot)

            act.wait_ge(eb_full, 2 * EDGE_GROUPS)
            act.wait_ge(meta_out, 3 * DMA)

            def load(b, k, full, use):
                n = P if full else NP
                need = [act.value_load(needs_dram[bass.ds(b, 1), odd:odd + 1], min_val=1, max_val=LAYER_ROWS[odd])
                        for odd in range(2)]
                act.wait_ge(out_stored[k], DMA * use)
                for odd in range(2):
                    act.wait_ge(scattered[1][odd], need[odd])
                x_at = blocks(x, RI)[b] if full else rows_left(x)
                r_at = blocks(root[1], RI)[b] if full else rows_left(root[1])
                act.dma_start(last_x[k][0:n, :], x_at).then_inc(last_in[k], DMA)
                act.dma_start(last_root[k][0:n, :], r_at).then_inc(last_in[k], DMA)

            def finish(b, k, n):
                act.wait_ge(spread, b + 1)
                nc.scalar.activation(small[0:n, 3, :], small[0:n, 2, :], ACT.Sqrt, bias=eps[0:n, 0:1]).then_inc(summed, 1)
                act.wait_ge(scaled, b + 1)
                for i in range(RI - ACT_TILES, RI):
                    at = slice(i * D, (i + 1) * D)
                    last = nc.scalar.activation(last_root[k][0:n, at], last_x[k][0:n, at], ACT.Identity,
                                                bias=small[0:n, 5, i:i + 1], scale=small[0:n, 4, i:i + 1])
                last.then_inc(act_normed, 1)
                act.wait_ge(act_normed, b + 1)
                act.wait_ge(vec_normed, b + 1)

            def store(b, k, full):
                n = P if full else NP
                to = blocks(out, RI)[b] if full else rows_left(out)
                act.dma_start(to, last_root[k][0:n, :]).then_inc(out_stored[k], DMA)

            load(0, 0, True, 0)
            load(1, 1, True, 0)
            def full_blocks(it):
                for k in range(NB_OUT):
                    b = NB_OUT * it + k
                    finish(b, k, P)
                    store(b, k, True)
                    load(b + 2, (k + 2) % NB_OUT, True, it + (k + 2) // NB_OUT)

            full_blocks(0)
            with act.Fori(1, NBL // NB_OUT - 1) as it:
                full_blocks(it)
            for b in range(NBL - NB_OUT, BLOCKS):
                k = b % NB_OUT
                finish(b, k, P if b < NBL else NP)
                store(b, k, b < NBL)
                if b + 2 < BLOCKS:
                    load(b + 2, (b + 2) % NB_OUT, b + 2 < NBL, (b + 2) // NB_OUT)
            for k in range(NB_OUT):
                act.wait_ge(out_stored[k], DMA * ((BLOCKS - k + NB_OUT - 1) // NB_OUT))

        @block.vector
        def _(dve):
            nc.vector.memset(src_all[:, NSB * RI:], 0).then_inc(preset, 1)
            nc.vector.memset(next_dst, -1).then_inc(preset, 1)
            nc.vector.memset(prev_dst, -1).then_inc(preset, 1)
            nc.vector.memset(zero_rows, 0.0).then_inc(zeroed, 1)
            nc.vector.memset(nodes_t[D:D + 1, :, :], 1.0)
            nc.vector.memset(eps[:], EPS)
            nc.vector.memset(slopes[0:D, :], SLOPE)
            nc.vector.memset(slopes[D:K, :], 1.0)
            nc.vector.memset(msgs[1][0:D, SB - 1:SB], -BIG).then_inc(zeroed, 1)

            def stage_src(s, odd, before):
                dve.wait_ge(rows_in[odd], before)
                nc.vector.tensor_copy(src_now[:, odd, :], src_all[:, bass.ds(s * RI, RI)]).then_inc(src_staged[odd], 1)

            def link(ins):
                link.n += 1
                ins.then_inc(meta_step, 1)
                dve.wait_ge(meta_step, link.n)
            link.n = 0

            def metadata():
                dve.wait_ge(dst_in, 6 * DMA)
                dve.wait_ge(numbered, 3)
                link(nc.vector.tensor_tensor(same_next, this_dst, next_dst, ALU.is_equal))
                link(nc.vector.tensor_scalar(number, number, SPARE - 1, None, ALU.bitwise_and))
                link(nc.vector.tensor_scalar(spare, number, float(N), None, ALU.add))
                link(nc.vector.tensor_tensor(step, spare, this_dst, ALU.subtract))
                link(nc.vector.tensor_tensor(step, step, same_next, ALU.mult))
                link(nc.vector.tensor_tensor(target, step, this_dst, ALU.add))
                link(nc.vector.tensor_tensor(same_prev, this_dst, prev_dst, ALU.is_equal))
                link(nc.vector.tensor_scalar(same_prev, same_prev, -0.5, 2.0, ALU.add, ALU.mult))
                link(nc.vector.tensor_scalar(keep_all, same_prev, BIG, None, ALU.mult))
                link(nc.vector.tensor_copy(bound[:], bound_i[:]))
                link(nc.vector.memset(share[:], 0.0))
                link(nc.vector.memset(share[:, 0, 0:NSB:2], float(RI * DMA)))
                link(nc.vector.memset(share[:, 1, 1:NSB:2], float(RI * DMA)))
                link(nc.vector.memset(share[:, 0, NSB:NSB + 1], float(EJ * DMA)))
                for odd in range(2):
                    link(nc.vector.tensor_scalar(below[0:BLOCKS, odd, :], first[0:BLOCKS, :], bound[0:BLOCKS, 0:1],
                                                 None, ALU.is_lt))
                    link(nc.vector.tensor_tensor(below[0:BLOCKS, odd, :], below[0:BLOCKS, odd, :],
                                                 share[0:BLOCKS, odd, :], ALU.mult))
                    link(nc.vector.tensor_reduce(needs_f[0:BLOCKS, odd:odd + 1], below[0:BLOCKS, odd, :], AX_X, ALU.add))
                link(nc.vector.tensor_scalar(needs[0:BLOCKS, :], needs_f[0:BLOCKS, :], 1.0, None, ALU.max))
                assert link.n == META_STEPS

            def place_attr(t):
                dve.wait_ge(attr_in, DMA * (t.order + 1))
                dve.wait_ge(edges_turned[t.odd], t.use)
                nc.vector.tensor_copy(gathered[t.odd][0:t.ep, 0:t.ej, D:K],
                                      attr[0:t.ep, 0:t.ej * DE].rearrange("p (r k) -> p r k", k=DE),
                                      ).then_inc(attr_placed, 1)

            def leaky_nodes(t, j):
                bank, cols = j % 2, slice(0, GROUP * t.np)
                dve.wait_ge(nt_scaled[bank], t.ngroup_use(j) - BLOCKS * (NG // 2) + 1)
                nc.vector.tensor_tensor(nodes_t[0:D, bank, cols], nt_ps[bank][0:D, cols], nodes_t[0:D, bank, cols],
                                        ALU.max).then_inc(nt_free[bank], 1)

            def leaky_edges(t, q):
                bank, cols = q % 2, slice(0, GROUP * t.ep)
                dve.wait_ge(et_scaled[bank], t.egroup_use(q) - EDGE_GROUPS // 2 + 1)
                nc.vector.tensor_tensor(edges_t[:, cols], et_ps[bank][:, cols], edges_t[:, cols],
                                        ALU.max).then_inc(et_free[bank], 1)

            def read_root(t, j):
                root_to_sbuf(dve, t, j)(nc.vector.tensor_copy)

            def scan(t, c):
                if c == 0:
                    dve.wait_ge(scanned, t.order)
                    dve.wait_ge(em_free, t.egroup(t.egroups))
                    dve.wait_ge(keep_in, DMA * (t.order + 1))
                    start = msgs[1 - t.odd][0:D, SB - 1:SB]
                else:
                    start = msgs[t.odd][0:D, c * SCAN - 1:c * SCAN]
                    dve.wait_ge(scan_part, t.scan_parts() + c)
                at = slice(c * SCAN, min((c + 1) * SCAN, t.cols))
                ins = nc.vector.tensor_tensor_scan(msgs[t.odd][0:D, at], keep[0:D, at], msgs[t.odd][0:D, at],
                                                   start, ALU.min, ALU.max)
                ins.then_inc(scanned if at.stop == t.cols else scan_part, 1)

            def read_back(t, q):
                dve.wait_ge(eb_full, t.egroup(q) + 1)
                if t.full:
                    to = hold[:, bass.ds(t.s * RI + q * GROUP, GROUP), :]
                else:
                    to = hold[0:EP, NSB * RI + q * GROUP:NSB * RI + (q + 1) * GROUP, :]
                nc.vector.tensor_copy(to, eb_ps[0:t.ep, 0:GROUP * D].rearrange("p (r d) -> p r d", d=D)).then_inc(eb_free, 1)

            def slot(t):
                place_attr(t)
                scans = -(-t.cols // SCAN)
                for j in range(t.ngroups + 1):
                    if t.layer and j < t.ngroups:
                        leaky_nodes(t, j)
                    if t.layer and j < t.egroups:
                        leaky_edges(t, j)
                    if j == 0 and t.full:
                        stage_src(t.s + 2, t.odd, t.rows())
                    if not t.layer and j >= 1:
                        read_root(t, j - 1)
                    if j > t.egroups and j - t.egroups - 1 < scans:
                        scan(t, j - t.egroups - 1)
                for q in range(t.egroups):
                    read_back(t, q)

            dve.wait_ge(src_in, 2 * DMA)
            for layer in range(2):
                if layer == 0:
                    stage_src(0, 0, 0)
                    stage_src(1, 1, 0)
                    metadata()
                    dve.wait_ge(meta_out, 3 * DMA)
                    dve.wait_ge(spare_zeroed, 2 * (SPARE // SB) * DMA)
                else:
                    stage_src(0, 0, LAYER_ROWS[0])
                    stage_src(1, 1, LAYER_ROWS[1])
                slots(dve, layer, slot)

            def norm(b, k, n, use):
                mean, half_diff, var, dev, inv, shift = (small[0:n, i, :] for i in range(6))
                step0 = b * NORM_STEPS
                def step_of(ins, i):
                    ins.then_inc(vec_step, 1)
                    dve.wait_ge(vec_step, step0 + i + 1)

                dve.wait_ge(last_in[k], 2 * DMA * (use + 1))
                y, r = last_x[k], last_root[k]
                step_of(nc.vector.scalar_tensor_tensor(r[0:n, :], r[0:n, :], SLOPE, r[0:n, :], ALU.mult, ALU.max), 0)
                step_of(nc.vector.tensor_tensor(y[0:n, :], y[0:n, :], r[0:n, :], ALU.add), 1)
                for i in range(RI):
                    last = nc.vector.bn_stats(stats[0:n, i, :], y[0:n, i * D:(i + 1) * D])
                step_of(last, 2)
                even, odd = stats[0:n, :, 1], stats[0:n, :, 4]
                nc.vector.tensor_tensor(mean, even, odd, ALU.add)
                step_of(nc.vector.tensor_tensor(half_diff, even, odd, ALU.subtract), 3)
                nc.vector.tensor_scalar(mean, mean, 0.5, None, ALU.mult)
                nc.vector.tensor_tensor(var, stats[0:n, :, 2], stats[0:n, :, 5], ALU.add)
                step_of(nc.vector.scalar_tensor_tensor(half_diff, half_diff, 0.25, half_diff, ALU.mult, ALU.mult), 4)
                nc.vector.scalar_tensor_tensor(var, var, 1.0 / D, half_diff, ALU.mult, ALU.add).then_inc(spread, 1)
                dve.wait_ge(summed, b + 1)
                dve.wait_ge(act_normed, b)
                step_of(nc.vector.reciprocal(inv, dev), 5)
                nc.vector.scalar_tensor_tensor(shift, mean, -1.0, inv, ALU.mult, ALU.mult).then_inc(scaled, 1)
                for i in range(RI - ACT_TILES):
                    at = slice(i * D, (i + 1) * D)
                    last = nc.vector.tensor_scalar(last_root[k][0:n, at], y[0:n, at], small[0:n, 0, i:i + 1],
                                                   small[0:n, 4, i:i + 1], ALU.subtract, ALU.mult)
                last.then_inc(vec_normed, 1)

            for k in range(NB_OUT):
                norm(k, k, P, 0)
            with dve.Fori(1, NBL // NB_OUT) as it:
                for k in range(NB_OUT):
                    norm(NB_OUT * it + k, k, P, it)
            norm(NBL, NBL % NB_OUT, NP, NBL // NB_OUT)


_WEIGHTS = [f"L0_gnn_{w}" for w in ("W1_msg", "W1_edge", "W1_root", "b1", "W2_msg", "W2_edge", "W2_root", "b2")]
_INS = ["x", "src", "dst", "edge_attr_32"] + _WEIGHTS


def kernel(**inputs):
    import numpy as _np
    import concourse.bacc as _bacc
    from concourse import mybir as _mybir
    from concourse.bass_utils import run_bass_kernel_spmd as _run

    nc = _bacc.Bacc("TRN2", target_bir_lowering=False, num_devices=1, dynamic_dma_scratch_size=8192)
    arrays, args = {}, []
    for name in _INS:
        a = _np.ascontiguousarray(inputs[name])
        arrays[f"in_{name}_dram"] = a
        args.append(nc.dram_tensor(f"in_{name}_dram", a.shape, _mybir.dt.from_np(a.dtype), kind="ExternalInput").ap())
    shape = inputs["x"].shape
    out = nc.dram_tensor("out_0_dram", tuple(shape), _mybir.dt.float32, kind="ExternalOutput").ap()
    gnn(nc, *args[:4], args[4:], out)
    r = _run(nc, [arrays], core_ids=[0])
    return r.results[0]["out_0_dram"]
```

```python
from contextlib import ExitStack

import concourse.bass as bass
from concourse import mybir

F32 = mybir.dt.float32
BF16 = mybir.dt.bfloat16
I32 = mybir.dt.int32
ALU = mybir.AluOpType
ACT = mybir.ActivationFunctionType
AX_X = mybir.AxisListType.X

P = 128
GROUP = 4
RI = 16
SB = P * RI
SPARE = 2 * SB
SLOPE = 0.01
EPS = 1e-5
BIG = 3.3895313892515355e38
DMA = 16
NB_OUT = 3
ACT_TILES = 6
META_STEPS = 21
NORM_STEPS = 6
BACK_STEP = 1
SCAN = GROUP * P


def gnn(nc, x, src, dst, edge_attr, weights, out):
    N, D = x.shape
    E, DE = edge_attr.shape
    K = D + DE
    NSB, E_LEFT = divmod(E, SB)
    NBL, N_LEFT = divmod(N, SB)
    EJ = 8
    EP, NP = E_LEFT // EJ, N_LEFT // RI
    assert K == P and EP * EJ == E_LEFT and NP * RI == N_LEFT and EP <= P and NP <= P
    assert NSB % 2 == 0 and NBL == 2 * NSB and NBL % NB_OUT == 0
    HALF = RI // 2
    NG = RI // GROUP
    EG_LEFT = EJ // GROUP
    SB_USES = (NSB // 2 + 1, NSB // 2)
    EDGE_GROUPS = NSB * NG + EG_LEFT
    BLOCKS = NBL + 1
    MP = 125
    MC = E // MP
    assert MP * MC == E

    with ExitStack() as ctx:
        def sb(name, shape, dt):
            return ctx.enter_context(nc.sbuf_tensor(name, shape, dt))

        def psum(name, shape):
            return ctx.enter_context(nc.psum_tensor(name, shape, F32))

        def sem(name):
            return ctx.enter_context(nc.semaphore(name))

        def sems(name, n=2):
            return [sem(f"{name}{i}") for i in range(n)]

        root = [nc.dram_tensor(f"root{i}", (N + SPARE, D), F32, kind="Internal").ap() for i in range(2)]
        rows_to_dram = nc.dram_tensor("scatter_rows", (E,), I32, kind="Internal").ap()
        keep_dram = nc.dram_tensor("keep_row", (E,), BF16, kind="Internal").ap()
        needs_dram = nc.dram_tensor("needs_table", (BLOCKS, 2), I32, kind="Internal").ap()

        hold = sb("hold", [P, NSB * RI + EJ, D], F32)
        shared = sb("shared", [P, 6 * RI * D], F32)
        nodes_in = sb("nodes_in", [P, 2, RI * D], F32)
        root_out = sb("root_out", [P, 2, HALF * D], F32)
        nodes_t = sb("nodes_t", [P, 2, GROUP * P], F32)
        edges_t = sb("edges_t", [P, GROUP * P], F32)
        attr = sb("attr", [P, RI * DE], F32)
        ident = sb("ident", [P, P], F32)
        w_root = sb("w_root", [P, 2, D], F32)
        w_edge = sb("w_edge", [P, 2, D], F32)
        src_all = sb("src_all", [P, (NSB + 2) * RI], I32)
        src_now = sb("src_now", [P, 2, RI], I32)
        rows_now = sb("rows_now", [P, 2, RI], I32)
        stats = sb("stats", [P, RI, 6], F32)
        small = sb("small", [P, 6, RI], F32)
        slopes = sb("slopes", [P, 1], F32)
        eps = sb("eps", [P, 1], F32)
        first = sb("first", [P, NSB + 1], I32)
        below = sb("below", [P, 2, NSB + 1], F32)
        share = sb("share", [P, 2, NSB + 1], F32)
        bound_i = sb("bound_i", [P, 1], I32)
        bound = sb("bound", [P, 1], F32)
        needs = sb("needs", [P, 2], I32)
        needs_f = sb("needs_f", [P, 2], F32)

        gathered = [shared[:, i * RI * K:(i + 1) * RI * K].rearrange("p (r k) -> p r k", k=K) for i in range(2)]
        msgs = [shared[:, (2 + i) * SB:(3 + i) * SB] for i in range(2)]
        keep = shared[:, 4 * SB:4 * SB + SB // 2].bitcast(BF16)
        last_root = [shared[:, i * RI * D:(i + 1) * RI * D] for i in range(NB_OUT)]
        last_x = [shared[:, (NB_OUT + i) * RI * D:(NB_OUT + i + 1) * RI * D] for i in range(NB_OUT)]

        flat = hold[:].rearrange("p t d -> p (t d)")
        meta_at = (NSB * RI + EJ) * D

        def meta(i, dt):
            a = flat[0:MP, meta_at - (i + 1) * MC:meta_at - i * MC]
            return a if dt is F32 else a.bitcast(dt)

        this_dst, next_dst, prev_dst, number = (meta(i, I32) for i in range(4))
        same_next, same_prev, spare, step = (meta(4 + i, F32) for i in range(4))
        target = meta(8, I32)
        keep_all = flat[0:MP, meta_at - 9 * MC - MC // 2:meta_at - 9 * MC].bitcast(BF16)
        zero_rows = flat[:, 0:RI * D]

        nt_ps = [psum(f"nt_ps{i}", [P, GROUP * P]) for i in range(2)]
        no_ps = [psum(f"no_ps{i}", [P, GROUP * P]) for i in range(2)]
        et_ps = [psum(f"et_ps{i}", [P, GROUP * P]) for i in range(2)]
        em_ps = psum("em_ps", [P, GROUP * P])
        eb_ps = psum("eb_ps", [P, GROUP * P])

        zeroed, ident_done, weights_in, src_in = sem("zeroed"), sem("ident_done"), sem("weights_in"), sem("src_in")
        preset, dst_in, meta_step, meta_out = sem("preset"), sem("dst_in"), sem("meta_step"), sem("meta_out")
        numbered, spare_zeroed = sem("numbered"), sem("spare_zeroed")
        block_in, block_turned = sems("block_in"), sems("block_turned")
        nt_full, nt_free, nt_scaled = sems("nt_full", NG - 1), sems("nt_free"), sems("nt_scaled")
        no_full, no_free = sems("no_full"), sems("no_free")
        root_stored = sems("root_stored")
        src_staged, rows_in, edges_turned = sems("src_staged"), sems("rows_in"), sems("edges_turned")
        attr_in, attr_placed = sem("attr_in"), sem("attr_placed")
        et_full, et_free, et_scaled = sems("et_full", NG - 1), sems("et_free"), sems("et_scaled")
        em_full, em_free = sem("em_full"), sem("em_free")
        keep_in, scan_part, scanned = sem("keep_in"), sem("scan_part"), sem("scanned")
        eb_full, eb_free = sem("eb_full"), sem("eb_free")
        pool_open = sem("pool_open")
        rows_staged = sems("rows_staged")
        staged, scattered = sems("staged"), [sems("scattered_a"), sems("scattered_b")]
        last_in = sems("last_in", NB_OUT)
        summed, spread = sem("summed"), sem("spread")
        vec_step, scaled, vec_normed = sem("vec_step"), sem("scaled"), sem("vec_normed")
        act_normed, out_stored = sem("act_normed"), sems("out_stored", NB_OUT)

        def blocks(a, width):
            return a[0:NBL * SB, :].rearrange("(b p r) d -> b p (r d)", p=P, r=width)

        def rows_left(a):
            return a[NBL * SB:N, :].rearrange("(p r) d -> p (r d)", r=RI)

        h_of = [x, root[0]]
        src_full = src[0:NSB * SB].rearrange("(s p r) -> p s r", p=P, r=RI)
        src_left = src[NSB * SB:E].rearrange("(p r) -> p r", r=EJ)
        to_full = rows_to_dram[0:NSB * SB].rearrange("(s p r) -> s p r", p=P, r=RI)
        to_left = rows_to_dram[NSB * SB:E].rearrange("(p r) -> p r", r=EJ)
        attr_full = edge_attr[0:NSB * SB, :].rearrange("(s p r) d -> s p (r d)", p=P, r=RI)
        attr_left = edge_attr[NSB * SB:E, :].rearrange("(p r) d -> p (r d)", r=EJ)
        keep_full = keep_dram[0:NSB * SB].rearrange("(s a e) -> s a e", s=NSB, a=1)
        keep_left = keep_dram[NSB * SB:E].rearrange("(a e) -> a e", a=1)
        dst_row = dst.rearrange("(a e) -> a e", a=1)

        LAYER_ROWS = ((NSB // 2 * RI + EJ) * DMA, NSB // 2 * RI * DMA)

        class Slot:

            def __init__(self, layer, it, odd):
                self.layer, self.odd, self.full = layer, odd, it is not None
                self.s = 2 * it + odd if self.full else NSB
                self.half = it if self.full else NSB // 2
                self.use = layer * SB_USES[odd] + self.half
                self.order = layer * (NSB + 1) + self.s
                self.ep, self.ej = (P, RI) if self.full else (EP, EJ)
                self.egroups = NG if self.full else EG_LEFT
                self.cols = self.ep * self.ej
                self.np = P if self.full else NP
                self.nblocks = 2 if self.full else 1
                self.ngroups = NG * self.nblocks

            def block(self, k):
                return 2 * self.s + k

            def block_use(self, k):
                return self.layer * (NSB + (1 if k == 0 else 0)) + self.s

            def ngroup_use(self, j):
                return self.layer * BLOCKS * (NG // 2) + self.block(j // NG) * (NG // 2) + (j % NG) // 2

            def root_use(self, j):
                return self.layer * BLOCKS + self.block(j // NG)

            def egroup_use(self, q):
                return self.layer * (EDGE_GROUPS // 2) + self.s * (NG // 2) + q // 2

            def egroup(self, q):
                return self.layer * EDGE_GROUPS + self.s * NG + q

            def rows(self):
                return self.layer * LAYER_ROWS[self.odd] + (self.half * RI + self.ej) * DMA

            def nodes_turned(self, j):
                if j % NG == NG - 1:
                    return block_turned[j // NG], self.block_use(j // NG) + 1
                return nt_full[j % NG], self.root_use(j) + 1

            def edges_turned(self, q):
                if q == self.egroups - 1:
                    return edges_turned[self.odd], self.use + 1
                return et_full[q], (self.order if q == 0 else self.layer * NSB + self.s) + 1

            def stages(self):
                if self.layer:
                    return SB_USES[self.odd] + (self.half + 1) * DMA
                return self.half + 1

            def scan_parts(self):
                return self.layer * (NSB * (NG - 1) + EG_LEFT - 1) + self.s * (NG - 1)

        def slots(body, eng, layer):
            for odd in range(2):
                body(Slot(layer, 0, odd))
            with eng.Fori(1, NSB // 2) as it:
                for odd in range(2):
                    body(Slot(layer, it, odd))
            body(Slot(layer, None, 0))

        def staggered(body, eng, layer):
            body(None, Slot(layer, 0, 0), None)
            body(Slot(layer, 0, 0), Slot(layer, 0, 1), None)
            body(Slot(layer, 0, 1), Slot(layer, 1, 0), Slot(layer, 0, 0))
            with eng.Fori(1, NSB // 2 - 1) as it:
                body(Slot(layer, it, 0), Slot(layer, it, 1), Slot(layer, it - 1, 1))
                body(Slot(layer, it, 1), Slot(layer, it + 1, 0), Slot(layer, it, 0))
            end = NSB // 2 - 1
            body(Slot(layer, end, 0), Slot(layer, end, 1), Slot(layer, end - 1, 1))
            body(Slot(layer, end, 1), Slot(layer, None, 0), Slot(layer, end, 0))
            body(Slot(layer, None, 0), None, Slot(layer, end, 1))
            body(None, None, Slot(layer, None, 0))

        def counts(t, n, back):
            groups = t.egroups if t else 0, n.ngroups if n else 0, back.egroups if back else 0
            return *groups, max(groups[0] + 1, groups[1] + 1, (BACK_STEP if t else 0) + groups[2])

        def stage(eng, t, copy):
            if isinstance(t.s, int) and t.s == 0:
                eng.wait_ge(block_turned[0], (t.layer + 1) * (NSB + 1))
                eng.wait_ge(block_turned[1], (t.layer + 1) * NSB)
            eng.wait_ge(eb_free, t.egroup(t.egroups))
            eng.wait_ge(scattered[t.layer][t.odd], t.half * RI * DMA)
            tiles = bass.ds(t.s * RI, t.ej)
            to, of = nodes_in[0:t.ep, t.odd, 0:t.ej * D], hold[0:t.ep, tiles, :].rearrange("p r d -> p (r d)")
            copy(to, of).then_inc(staged[t.odd], DMA if t.layer else 1)

        def root_to_sbuf(eng, t, j):
            bank, half = j % 2, (j % NG) // 2
            eng.wait_ge(no_full[bank], t.ngroup_use(j) + 1)
            if j % 2 == 0:
                eng.wait_ge(root_stored[half], DMA * t.root_use(j))
            at = slice((j % 2) * GROUP * D, (j % 2 + 1) * GROUP * D)
            to, of = root_out[0:t.np, half, at], no_ps[bank][0:t.np, 0:GROUP * D]
            return lambda copy: copy(to, of).then_inc(no_free[bank], 1)

        block = ctx.enter_context(nc.Block())

        @block.sync
        def _(sp):
            sp.dma_start(src_all[:, 0:NSB * RI].rearrange("p (s r) -> p s r", r=RI), src_full).then_inc(src_in, DMA)
            sp.wait_ge(preset, 1)
            sp.dma_start(src_all[0:EP, NSB * RI:NSB * RI + EJ], src_left).then_inc(src_in, DMA)
            for layer in range(2):
                w_msg, w_e, w_r, bias = weights[4 * layer:4 * layer + 4]
                sp.dma_start(w_edge[0:D, layer, :], w_msg).then_inc(weights_in, DMA)
                sp.dma_start(w_edge[D:K, layer, :], w_e).then_inc(weights_in, DMA)
                sp.dma_start(w_root[0:D, layer, :], w_r).then_inc(weights_in, DMA)
                sp.dma_start(w_root[D:D + 1, layer, :], bias.rearrange("(a d) -> a d", a=1)).then_inc(weights_in, DMA)
            sp.dma_start(this_dst, dst.rearrange("(p c) -> p c", c=MC)).then_inc(dst_in, DMA)
            sp.wait_ge(preset, 3)
            last = (MP - 1) * MC
            sp.dma_start(next_dst[0:MP - 1, :], dst[1:last + 1].rearrange("(p c) -> p c", c=MC)).then_inc(dst_in, DMA)
            sp.dma_start(next_dst[MP - 1:MP, 0:MC - 1], dst_row[:, last + 1:E]).then_inc(dst_in, DMA)
            sp.dma_start(prev_dst[0:1, 1:MC], dst_row[:, 0:MC - 1]).then_inc(dst_in, DMA)
            sp.dma_start(prev_dst[1:MP, :], dst[MC - 1:E - 1].rearrange("(p c) -> p c", c=MC)).then_inc(dst_in, DMA)
            with nc.allow_non_contiguous_dma(reason="the first dst of each superblock"):
                sp.dma_start(first[0:BLOCKS, :], dst_row[:, 0:E:SB].to_broadcast([BLOCKS, NSB + 1])).then_inc(dst_in, DMA)
            sp.wait_ge(zeroed, 1)
            for layer in range(2):
                for i in range(SPARE // SB):
                    to = root[layer][N + i * SB:N + (i + 1) * SB, :].rearrange("(p r) d -> p (r d)", r=RI)
                    sp.dma_start(to, zero_rows).then_inc(spare_zeroed, DMA)
            sp.wait_ge(meta_step, META_STEPS)
            sp.dma_start(rows_to_dram.rearrange("(p c) -> p c", c=MC), target).then_inc(meta_out, DMA)
            sp.dma_start(keep_dram.rearrange("(p c) -> p c", c=MC), keep_all).then_inc(meta_out, DMA)
            sp.dma_start(needs_dram, needs[0:BLOCKS, :]).then_inc(meta_out, DMA)

            def loads(t):
                h = h_of[t.layer]
                for k in range(t.nblocks):
                    sp.wait_ge(block_turned[k], t.block_use(k))
                    if t.full:
                        sp.dma_start(nodes_in[:, k, :], blocks(h, RI)[t.block(k)]).then_inc(block_in[k], DMA)
                    else:
                        sp.dma_start(nodes_in[0:NP, k, :], rows_left(h)).then_inc(block_in[k], DMA)
                    if k == 0:
                        sp.wait_ge(attr_placed, t.order)
                        if t.full:
                            sp.dma_start(attr[:], attr_full[t.s]).then_inc(attr_in, DMA)
                        else:
                            sp.dma_start(attr[0:EP, 0:EJ * DE], attr_left).then_inc(attr_in, DMA)

            def load_rows(t):
                if t.layer:
                    stage(sp, t, sp.dma_start)
                sp.wait_ge(scattered[t.layer][t.odd], t.half * RI * DMA)
                if t.full:
                    sp.dma_start(rows_now[:, t.odd, :], to_full[t.s]).then_inc(rows_staged[t.odd], DMA)
                else:
                    sp.dma_start(rows_now[0:EP, t.odd, 0:EJ], to_left).then_inc(rows_staged[t.odd], DMA)

            for layer in range(2):
                slots(loads, sp, layer)
                slots(load_rows, sp, layer)
                if layer == 0:
                    for odd in range(2):
                        sp.wait_ge(scattered[0][odd], LAYER_ROWS[odd])

        @block.gpsimd
        def _(pool):
            nc.gpsimd.memset(ident[:], 0.0).then_inc(numbered, 1)
            pool.wait_ge(numbered, 1)
            nc.gpsimd.affine_select(out=ident[:], in_=ident[:], compare_op=ALU.not_equal, fill=1.0, base=0,
                                    pattern=[[-1, P]], channel_multiplier=1).then_inc(ident_done, 1)
            nc.gpsimd.iota(number, pattern=[[1, MC]], base=0, channel_multiplier=MC).then_inc(numbered, 1)
            nc.gpsimd.iota(bound_i[:], pattern=[[0, 1]], base=SB, channel_multiplier=SB).then_inc(numbered, 1)

            def gather(t):
                pool.wait_ge(src_staged[t.odd], t.layer * SB_USES[0] + t.half + 1)
                pool.wait_ge(edges_turned[t.odd], t.use)
                pool.sem_inc(pool_open, 1)
                for i in range(t.ej):
                    nc.gpsimd.indirect_dma_start(
                        out=gathered[t.odd][0:t.ep, i, 0:D], out_offset=None, in_=h_of[t.layer],
                        in_offset=bass.IndirectOffsetOnAxis(ap=src_now[0:t.ep, t.odd, i:i + 1], axis=0),
                    ).then_inc(rows_in[t.odd], DMA)

            def scatter(t):
                pool.wait_ge(staged[t.odd], t.stages())
                pool.wait_ge(rows_staged[t.odd], DMA * (t.use + 1))
                pool.sem_inc(pool_open, 1)
                for i in range(t.ej):
                    nc.gpsimd.indirect_dma_start(
                        out=root[t.layer],
                        out_offset=bass.IndirectOffsetOnAxis(ap=rows_now[0:t.ep, t.odd, i:i + 1], axis=0),
                        in_=nodes_in[0:t.ep, t.odd, i * D:(i + 1) * D], in_offset=None, compute_op=ALU.add,
                    ).then_inc(scattered[t.layer][t.odd], DMA)

            for layer in range(2):
                slots(gather, pool, layer)
                pool.wait_ge(spare_zeroed, 2 * (SPARE // SB) * DMA)
                for half in range(2):
                    pool.wait_ge(root_stored[half], (layer + 1) * BLOCKS * DMA)
                slots(scatter, pool, layer)
                for odd in range(2):
                    pool.wait_ge(scattered[layer][odd], LAYER_ROWS[odd])

        @block.tensor
        def _(pe):
            pe.wait_ge(ident_done, 1)
            pe.wait_ge(weights_in, 8 * DMA)
            pe.wait_ge(zeroed, 2)

            def turn_nodes(t, j):
                k, g, bank = j // NG, j % NG, j % 2
                if g == 0:
                    pe.wait_ge(block_in[k], DMA * (t.block_use(k) + 1))
                pe.wait_ge(nt_free[bank], t.ngroup_use(j))
                for i in range(GROUP):
                    at = (g * GROUP + i) * D
                    last = nc.tensor.transpose(nt_ps[bank][0:D, i * t.np:(i + 1) * t.np],
                                               nodes_in[0:t.np, k, at:at + D], ident[0:t.np, 0:t.np])
                last.then_inc(t.nodes_turned(j)[0], 1)

            def root_of(t, j):
                bank = j % 2
                pe.wait_ge(nt_free[bank], t.ngroup_use(j) + 1)
                pe.wait_ge(no_free[bank], t.ngroup_use(j))
                for i in range(GROUP):
                    last = nc.tensor.matmul(no_ps[bank][0:t.np, i * D:(i + 1) * D],
                                            nodes_t[0:D + 1, bank, i * t.np:(i + 1) * t.np],
                                            w_root[0:D + 1, t.layer, :], start=True, stop=True)
                last.then_inc(no_full[bank], 1)

            def turn_edges(t, q):
                bank = q % 2
                if q == 0:
                    pe.wait_ge(rows_in[t.odd], t.rows())
                    pe.wait_ge(attr_placed, t.order + 1)
                pe.wait_ge(et_free[bank], t.egroup_use(q))
                for i in range(GROUP):
                    last = nc.tensor.transpose(et_ps[bank][:, i * t.ep:(i + 1) * t.ep],
                                               gathered[t.odd][0:t.ep, q * GROUP + i, :], ident[0:t.ep, 0:t.ep])
                last.then_inc(t.edges_turned(q)[0], 1)

            def messages(t, q):
                bank = q % 2
                pe.wait_ge(et_free[bank], t.egroup_use(q) + 1)
                pe.wait_ge(em_free, t.egroup(q))
                ins = nc.tensor.matmul(em_ps[0:D, 0:GROUP * t.ep], w_edge[:, t.layer, :],
                                       edges_t[:, 0:GROUP * t.ep], start=True, stop=True)
                ins.then_inc(em_full, 1)

            def turn_back(t, q):
                pe.wait_ge(scanned, t.order + 1)
                pe.wait_ge(eb_free, t.egroup(q))
                for i in range(GROUP):
                    cols = msgs[t.odd][0:D, q * GROUP + i:t.cols:t.ej]
                    last = nc.tensor.transpose(eb_ps[0:t.ep, i * D:(i + 1) * D], cols, ident[0:D, 0:D])
                last.then_inc(eb_full, 1)

            def slot(t, n, back):
                egroups, ngroups, bgroups, steps = counts(t, n, back)
                first_back = BACK_STEP if t else 0
                for j in range(steps):
                    if j < egroups:
                        turn_edges(t, j)
                    if j < ngroups:
                        turn_nodes(n, j)
                    if 1 <= j <= egroups:
                        messages(t, j - 1)
                    if 1 <= j <= ngroups:
                        root_of(n, j - 1)
                    if 0 <= j - first_back < bgroups:
                        turn_back(back, j - first_back)

            for layer in range(2):
                staggered(slot, pe, layer)

        @block.scalar
        def _(act):
            act.wait_ge(meta_out, 3 * DMA)

            def read_nodes(t, j):
                bank = j % 2
                act.wait_ge(*t.nodes_turned(j))
                act.wait_ge(no_full[bank], t.ngroup_use(j))
                cols = slice(0, GROUP * t.np)
                nc.scalar.activation(nodes_t[0:D, bank, cols], nt_ps[bank][0:D, cols], ACT.Copy,
                                     scale=SLOPE if t.layer else 1.0,
                                     ).then_inc((nt_scaled if t.layer else nt_free)[bank], 1)

            def read_edges(t, q):
                bank = q % 2
                act.wait_ge(*t.edges_turned(q))
                act.wait_ge(em_full, t.egroup(q))
                cols = slice(0, GROUP * t.ep)
                nc.scalar.activation(edges_t[:, cols], et_ps[bank][:, cols], ACT.Copy,
                                     scale=slopes[:, 0:1] if t.layer else 1.0,
                                     ).then_inc((et_scaled if t.layer else et_free)[bank], 1)

            def read_messages(t, q):
                act.wait_ge(em_full, t.egroup(q) + 1)
                if q == 0:
                    act.wait_ge(scanned, t.order)
                    view = keep_full[t.s] if t.full else keep_left
                    act.dma_start(keep[0:D, 0:t.cols], view.to_broadcast([D, t.cols])).then_inc(keep_in, DMA)
                to = msgs[t.odd][0:D, 0:t.cols].rearrange("d (p r) -> d p r", r=t.ej)[:, :, q * GROUP:(q + 1) * GROUP]
                nc.scalar.activation(to, em_ps[0:D, 0:GROUP * t.ep].rearrange("d (i p) -> d p i", i=GROUP),
                                     ACT.Copy).then_inc(em_free, 1)

            def read_root(t, j):
                root_to_sbuf(act, t, j)(nc.scalar.copy)

            def store_root(t, j):
                half = (j % NG) // 2
                act.wait_ge(no_free[0], t.ngroup_use(j - 1) + 1)
                act.wait_ge(no_free[1], t.ngroup_use(j) + 1)
                view = root[t.layer]
                at = slice(half * HALF * D, (half + 1) * HALF * D)
                if t.full:
                    to = blocks(view, RI)[t.block(j // NG)][:, at]
                else:
                    to = rows_left(view)[:, at]
                act.dma_start(to, root_out[0:t.np, half, :]).then_inc(root_stored[half], DMA)

            def slot(t, n, back):
                egroups, ngroups, bgroups, steps = counts(t, n, back)
                for j in range(steps):
                    if j < egroups:
                        read_edges(t, j)
                    if j < ngroups:
                        read_nodes(n, j)
                    if 1 <= j <= egroups:
                        read_messages(t, j - 1)
                    if 1 <= j <= ngroups:
                        if n.layer:
                            read_root(n, j - 1)
                        if j >= 3 and j % 2:
                            store_root(n, j - 2)
                if ngroups:
                    store_root(n, ngroups - 1)

            for layer in range(2):
                staggered(slot, act, layer)
                if layer == 0:
                    slots(lambda t: stage(act, t, nc.scalar.copy), act, layer)

            act.wait_ge(eb_full, 2 * EDGE_GROUPS)

            def load(b, k, full, use):
                n = P if full else NP
                need = [act.value_load(needs_dram[bass.ds(b, 1), odd:odd + 1], min_val=1, max_val=LAYER_ROWS[odd])
                        for odd in range(2)]
                act.wait_ge(out_stored[k], DMA * use)
                for odd in range(2):
                    act.wait_ge(scattered[1][odd], need[odd])
                x_at = blocks(x, RI)[b] if full else rows_left(x)
                r_at = blocks(root[1], RI)[b] if full else rows_left(root[1])
                act.dma_start(last_x[k][0:n, :], x_at).then_inc(last_in[k], DMA)
                act.dma_start(last_root[k][0:n, :], r_at).then_inc(last_in[k], DMA)

            def finish(b, k, n):
                act.wait_ge(spread, b + 1)
                nc.scalar.activation(small[0:n, 3, :], small[0:n, 2, :], ACT.Sqrt, bias=eps[0:n, 0:1]).then_inc(summed, 1)
                act.wait_ge(scaled, b + 1)
                for i in range(RI - ACT_TILES, RI):
                    at = slice(i * D, (i + 1) * D)
                    last = nc.scalar.activation(last_root[k][0:n, at], last_x[k][0:n, at], ACT.Identity,
                                                bias=small[0:n, 5, i:i + 1], scale=small[0:n, 4, i:i + 1])
                last.then_inc(act_normed, 1)
                act.wait_ge(act_normed, b + 1)
                act.wait_ge(vec_normed, b + 1)

            def store(b, k, full):
                n = P if full else NP
                to = blocks(out, RI)[b] if full else rows_left(out)
                act.dma_start(to, last_root[k][0:n, :]).then_inc(out_stored[k], DMA)

            load(0, 0, True, 0)
            load(1, 1, True, 0)
            def full_blocks(it):
                for k in range(NB_OUT):
                    b = NB_OUT * it + k
                    finish(b, k, P)
                    store(b, k, True)
                    load(b + 2, (k + 2) % NB_OUT, True, it + (k + 2) // NB_OUT)

            full_blocks(0)
            with act.Fori(1, NBL // NB_OUT - 1) as it:
                full_blocks(it)
            for b in range(NBL - NB_OUT, BLOCKS):
                k = b % NB_OUT
                finish(b, k, P if b < NBL else NP)
                store(b, k, b < NBL)
                if b + 2 < BLOCKS:
                    load(b + 2, (b + 2) % NB_OUT, b + 2 < NBL, (b + 2) // NB_OUT)
            for k in range(NB_OUT):
                act.wait_ge(out_stored[k], DMA * ((BLOCKS - k + NB_OUT - 1) // NB_OUT))

        @block.vector
        def _(dve):
            nc.vector.memset(src_all[:, NSB * RI:], 0).then_inc(preset, 1)
            nc.vector.memset(next_dst, -1).then_inc(preset, 1)
            nc.vector.memset(prev_dst, -1).then_inc(preset, 1)
            nc.vector.memset(zero_rows, 0.0).then_inc(zeroed, 1)
            nc.vector.memset(nodes_t[D:D + 1, :, :], 1.0)
            nc.vector.memset(eps[:], EPS)
            nc.vector.memset(slopes[0:D, :], SLOPE)
            nc.vector.memset(slopes[D:K, :], 1.0)
            nc.vector.memset(msgs[1][0:D, SB - 1:SB], -BIG).then_inc(zeroed, 1)

            def stage_src(s, odd, before):
                dve.wait_ge(rows_in[odd], before)
                nc.vector.tensor_copy(src_now[:, odd, :], src_all[:, bass.ds(s * RI, RI)]).then_inc(src_staged[odd], 1)

            def link(ins):
                link.n += 1
                ins.then_inc(meta_step, 1)
                dve.wait_ge(meta_step, link.n)
            link.n = 0

            def metadata():
                dve.wait_ge(dst_in, 6 * DMA)
                dve.wait_ge(numbered, 3)
                link(nc.vector.tensor_tensor(same_next, this_dst, next_dst, ALU.is_equal))
                link(nc.vector.tensor_scalar(number, number, SPARE - 1, None, ALU.bitwise_and))
                link(nc.vector.tensor_scalar(spare, number, float(N), None, ALU.add))
                link(nc.vector.tensor_tensor(step, spare, this_dst, ALU.subtract))
                link(nc.vector.tensor_tensor(step, step, same_next, ALU.mult))
                link(nc.vector.tensor_tensor(target, step, this_dst, ALU.add))
                link(nc.vector.tensor_tensor(same_prev, this_dst, prev_dst, ALU.is_equal))
                link(nc.vector.tensor_scalar(same_prev, same_prev, -0.5, 2.0, ALU.add, ALU.mult))
                link(nc.vector.tensor_scalar(keep_all, same_prev, BIG, None, ALU.mult))
                link(nc.vector.tensor_copy(bound[:], bound_i[:]))
                link(nc.vector.memset(share[:], 0.0))
                link(nc.vector.memset(share[:, 0, 0:NSB:2], float(RI * DMA)))
                link(nc.vector.memset(share[:, 1, 1:NSB:2], float(RI * DMA)))
                link(nc.vector.memset(share[:, 0, NSB:NSB + 1], float(EJ * DMA)))
                for odd in range(2):
                    link(nc.vector.tensor_scalar(below[0:BLOCKS, odd, :], first[0:BLOCKS, :], bound[0:BLOCKS, 0:1],
                                                 None, ALU.is_lt))
                    link(nc.vector.tensor_tensor(below[0:BLOCKS, odd, :], below[0:BLOCKS, odd, :],
                                                 share[0:BLOCKS, odd, :], ALU.mult))
                    link(nc.vector.tensor_reduce(needs_f[0:BLOCKS, odd:odd + 1], below[0:BLOCKS, odd, :], AX_X, ALU.add))
                link(nc.vector.tensor_scalar(needs[0:BLOCKS, :], needs_f[0:BLOCKS, :], 1.0, None, ALU.max))
                assert link.n == META_STEPS

            def place_attr(t):
                dve.wait_ge(attr_in, DMA * (t.order + 1))
                dve.wait_ge(edges_turned[t.odd], t.use)
                nc.vector.tensor_copy(gathered[t.odd][0:t.ep, 0:t.ej, D:K],
                                      attr[0:t.ep, 0:t.ej * DE].rearrange("p (r k) -> p r k", k=DE),
                                      ).then_inc(attr_placed, 1)

            def leaky_nodes(t, j):
                bank, cols = j % 2, slice(0, GROUP * t.np)
                dve.wait_ge(nt_scaled[bank], t.ngroup_use(j) - BLOCKS * (NG // 2) + 1)
                nc.vector.tensor_tensor(nodes_t[0:D, bank, cols], nt_ps[bank][0:D, cols], nodes_t[0:D, bank, cols],
                                        ALU.max).then_inc(nt_free[bank], 1)

            def leaky_edges(t, q):
                bank, cols = q % 2, slice(0, GROUP * t.ep)
                dve.wait_ge(et_scaled[bank], t.egroup_use(q) - EDGE_GROUPS // 2 + 1)
                nc.vector.tensor_tensor(edges_t[:, cols], et_ps[bank][:, cols], edges_t[:, cols],
                                        ALU.max).then_inc(et_free[bank], 1)

            def read_root(t, j):
                root_to_sbuf(dve, t, j)(nc.vector.tensor_copy)

            def scan(t, c):
                if c == 0:
                    dve.wait_ge(scanned, t.order)
                    dve.wait_ge(em_free, t.egroup(t.egroups))
                    dve.wait_ge(keep_in, DMA * (t.order + 1))
                    start = msgs[1 - t.odd][0:D, SB - 1:SB]
                else:
                    start = msgs[t.odd][0:D, c * SCAN - 1:c * SCAN]
                    dve.wait_ge(scan_part, t.scan_parts() + c)
                at = slice(c * SCAN, min((c + 1) * SCAN, t.cols))
                ins = nc.vector.tensor_tensor_scan(msgs[t.odd][0:D, at], keep[0:D, at], msgs[t.odd][0:D, at],
                                                   start, ALU.min, ALU.max)
                ins.then_inc(scanned if at.stop == t.cols else scan_part, 1)

            def read_back(t, q):
                dve.wait_ge(eb_full, t.egroup(q) + 1)
                if t.full:
                    to = hold[:, bass.ds(t.s * RI + q * GROUP, GROUP), :]
                else:
                    to = hold[0:EP, NSB * RI + q * GROUP:NSB * RI + (q + 1) * GROUP, :]
                nc.vector.tensor_copy(to, eb_ps[0:t.ep, 0:GROUP * D].rearrange("p (r d) -> p r d", d=D)).then_inc(eb_free, 1)

            def slot(t, n, back):
                egroups, ngroups, bgroups, steps = counts(t, n, back)
                first_back = BACK_STEP if t else 0
                scans = -(-t.cols // SCAN) if t else 0
                if t:
                    place_attr(t)
                for j in range(max(steps, egroups + 1 + scans)):
                    if (t or n or back).layer:
                        if j < egroups:
                            leaky_edges(t, j)
                        if j < ngroups:
                            leaky_nodes(n, j)
                    elif 1 <= j <= ngroups:
                        read_root(n, j - 1)
                    if j == 0 and t and t.full:
                        stage_src(t.s + 2, t.odd, t.rows())
                    if 0 <= j - first_back < bgroups:
                        read_back(back, j - first_back)
                    if 0 <= j - egroups - 1 < scans:
                        scan(t, j - egroups - 1)

            dve.wait_ge(src_in, 2 * DMA)
            for layer in range(2):
                if layer == 0:
                    stage_src(0, 0, 0)
                    stage_src(1, 1, 0)
                    metadata()
                    dve.wait_ge(meta_out, 3 * DMA)
                    dve.wait_ge(spare_zeroed, 2 * (SPARE // SB) * DMA)
                else:
                    stage_src(0, 0, LAYER_ROWS[0])
                    stage_src(1, 1, LAYER_ROWS[1])
                staggered(slot, dve, layer)

            def norm(b, k, n, use):
                mean, half_diff, var, dev, inv, shift = (small[0:n, i, :] for i in range(6))
                step0 = b * NORM_STEPS
                def step_of(ins, i):
                    ins.then_inc(vec_step, 1)
                    dve.wait_ge(vec_step, step0 + i + 1)

                dve.wait_ge(last_in[k], 2 * DMA * (use + 1))
                y, r = last_x[k], last_root[k]
                step_of(nc.vector.scalar_tensor_tensor(r[0:n, :], r[0:n, :], SLOPE, r[0:n, :], ALU.mult, ALU.max), 0)
                step_of(nc.vector.tensor_tensor(y[0:n, :], y[0:n, :], r[0:n, :], ALU.add), 1)
                for i in range(RI):
                    last = nc.vector.bn_stats(stats[0:n, i, :], y[0:n, i * D:(i + 1) * D])
                step_of(last, 2)
                even, odd = stats[0:n, :, 1], stats[0:n, :, 4]
                nc.vector.tensor_tensor(mean, even, odd, ALU.add)
                step_of(nc.vector.tensor_tensor(half_diff, even, odd, ALU.subtract), 3)
                nc.vector.tensor_scalar(mean, mean, 0.5, None, ALU.mult)
                nc.vector.tensor_tensor(var, stats[0:n, :, 2], stats[0:n, :, 5], ALU.add)
                step_of(nc.vector.scalar_tensor_tensor(half_diff, half_diff, 0.25, half_diff, ALU.mult, ALU.mult), 4)
                nc.vector.scalar_tensor_tensor(var, var, 1.0 / D, half_diff, ALU.mult, ALU.add).then_inc(spread, 1)
                dve.wait_ge(summed, b + 1)
                dve.wait_ge(act_normed, b)
                step_of(nc.vector.reciprocal(inv, dev), 5)
                nc.vector.scalar_tensor_tensor(shift, mean, -1.0, inv, ALU.mult, ALU.mult).then_inc(scaled, 1)
                for i in range(RI - ACT_TILES):
                    at = slice(i * D, (i + 1) * D)
                    last = nc.vector.tensor_scalar(last_root[k][0:n, at], y[0:n, at], small[0:n, 0, i:i + 1],
                                                   small[0:n, 4, i:i + 1], ALU.subtract, ALU.mult)
                last.then_inc(vec_normed, 1)

            for k in range(NB_OUT):
                norm(k, k, P, 0)
            with dve.Fori(1, NBL // NB_OUT) as it:
                for k in range(NB_OUT):
                    norm(NB_OUT * it + k, k, P, it)
            norm(NBL, NBL % NB_OUT, NP, NBL // NB_OUT)


_WEIGHTS = [f"L0_gnn_{w}" for w in ("W1_msg", "W1_edge", "W1_root", "b1", "W2_msg", "W2_edge", "W2_root", "b2")]
_INS = ["x", "src", "dst", "edge_attr_32"] + _WEIGHTS


def kernel(**inputs):
    import numpy as _np
    import concourse.bacc as _bacc
    from concourse import mybir as _mybir
    from concourse.bass_utils import run_bass_kernel_spmd as _run

    nc = _bacc.Bacc("TRN2", target_bir_lowering=False, num_devices=1, dynamic_dma_scratch_size=8192)
    arrays, args = {}, []
    for name in _INS:
        a = _np.ascontiguousarray(inputs[name])
        arrays[f"in_{name}_dram"] = a
        args.append(nc.dram_tensor(f"in_{name}_dram", a.shape, _mybir.dt.from_np(a.dtype), kind="ExternalInput").ap())
    shape = inputs["x"].shape
    out = nc.dram_tensor("out_0_dram", tuple(shape), _mybir.dt.float32, kind="ExternalOutput").ap()
    gnn(nc, *args[:4], args[4:], out)
    r = _run(nc, [arrays], core_ids=[0])
    return r.results[0]["out_0_dram"]
```

```python
from contextlib import ExitStack

import concourse.bass as bass
from concourse import mybir

F32 = mybir.dt.float32
BF16 = mybir.dt.bfloat16
I32 = mybir.dt.int32
ALU = mybir.AluOpType
ACT = mybir.ActivationFunctionType
AX_X = mybir.AxisListType.X

P = 128
GROUP = 4
RI = 16
SB = P * RI
SPARE = 2 * SB
SLOPE = 0.01
EPS = 1e-5
BIG = 3.3895313892515355e38
DMA = 16
LAST = 6
META_STEPS = 17
NORM_STEPS = 3
BACK_STEP = 1
SCAN = GROUP * P


def gnn(nc, x, src, dst, edge_attr, weights, out):
    N, D = x.shape
    E, DE = edge_attr.shape
    K = D + DE
    NSB, E_LEFT = divmod(E, SB)
    NBL, N_LEFT = divmod(N, SB)
    EJ = 8
    EP, NP = E_LEFT // EJ, N_LEFT // RI
    assert K == P and EP * EJ == E_LEFT and NP * RI == N_LEFT and EP <= P and NP <= P
    assert NSB % 2 == 0 and NBL == 2 * NSB and NBL % LAST == 0
    HALF = RI // 2
    NG = RI // GROUP
    EG_LEFT = EJ // GROUP
    SB_USES = (NSB // 2 + 1, NSB // 2)
    EDGE_GROUPS = NSB * NG + EG_LEFT
    BLOCKS = NBL + 1
    NEEDS = BLOCKS + 1
    MP = 125
    MC = E // MP
    assert MP * MC == E

    with ExitStack() as ctx:
        def sb(name, shape, dt):
            return ctx.enter_context(nc.sbuf_tensor(name, shape, dt))

        def psum(name, shape):
            return ctx.enter_context(nc.psum_tensor(name, shape, F32))

        def sem(name):
            return ctx.enter_context(nc.semaphore(name))

        def sems(name, n=2):
            return [sem(f"{name}{i}") for i in range(n)]

        root = [nc.dram_tensor(f"root{i}", (N + SPARE, D), F32, kind="Internal").ap() for i in range(2)]
        rows_to_dram = nc.dram_tensor("scatter_rows", (E,), I32, kind="Internal").ap()
        keep_dram = nc.dram_tensor("keep_row", (E,), BF16, kind="Internal").ap()
        needs_dram = nc.dram_tensor("needs_table", (NEEDS, 1), I32, kind="Internal").ap()

        hold = sb("hold", [P, NSB * RI + EJ, D], F32)
        shared = sb("shared", [P, 6 * RI * D], F32)
        nodes_in = sb("nodes_in", [P, 2, RI * D], F32)
        shared_2 = sb("shared_2", [P, 2 * RI * D], F32)
        attr = sb("attr", [P, RI * DE], F32)
        ident = sb("ident", [P, P], F32)
        w_root = sb("w_root", [P, 2, D], F32)
        w_edge = sb("w_edge", [P, 2, D], F32)
        src_all = sb("src_all", [P, (NSB + 2) * RI], I32)
        rows_all = sb("rows_all", [P, NSB * RI + EJ], I32)
        src_now = sb("src_now", [P, 2, RI], I32)
        rows_now = sb("rows_now", [P, 2, RI], I32)
        stats = sb("stats", [P, RI, 6], F32)
        small = sb("small", [P, 2, 6, RI], F32)
        slopes = sb("slopes", [P, 1], F32)
        eps = sb("eps", [P, 1], F32)
        bound_i = sb("bound_i", [P, 1], I32)
        needs_row = sb("needs_row", [1, NEEDS], I32)

        early = stats[:].rearrange("p r k -> p (r k)")
        ends, reach, share = (early[:, i * (NSB + 1):(i + 1) * (NSB + 1)] for i in range(3))
        ends = ends.bitcast(I32)
        bound, needs_f, needs = (early[:, i:i + 1] for i in range(3 * (NSB + 1), 3 * (NSB + 1) + 3))
        needs = needs.bitcast(I32)

        gathered = [shared[:, i * RI * K:(i + 1) * RI * K].rearrange("p (r k) -> p r k", k=K) for i in range(2)]
        msgs = [shared[:, (2 + i) * SB:(3 + i) * SB] for i in range(2)]
        keep = shared[:, 4 * SB:4 * SB + SB // 2].bitcast(BF16)
        middle_in = [shared[:, 2 * SB + i * RI * D:2 * SB + (i + 1) * RI * D] for i in range(2)]
        at_t = 2 * HALF * D
        root_out = shared_2[:, 0:at_t].rearrange("p (h c) -> p h c", h=2)
        nodes_t = shared_2[:, at_t:at_t + 2 * GROUP * P].rearrange("p (b c) -> p b c", b=2)
        edges_t = shared_2[:, at_t + 2 * GROUP * P:at_t + 3 * GROUP * P]
        assert at_t + 3 * GROUP * P == 2 * RI * D
        edges_t_of = [[edges_t], [edges_t, nodes_t[:, 0, :]]]
        last_root = [shared[:, i * RI * D:(i + 1) * RI * D] for i in range(3)]
        last_x = [nodes_in[:, i, :] for i in range(2)] + [shared[:, (3 + i) * RI * D:(4 + i) * RI * D] for i in range(3)]
        last_x.append(hold[:, (NSB - 2) * RI:(NSB - 1) * RI, :].rearrange("p r d -> p (r d)"))
        assert len(last_x) == LAST
        last_out = [shared_2[:, i * RI * D:(i + 1) * RI * D] for i in range(2)]

        flat = hold[:].rearrange("p t d -> p (t d)")
        meta_at = (NSB * RI + EJ) * D

        def meta(i, dt):
            a = flat[0:MP, meta_at - (i + 1) * MC:meta_at - i * MC]
            return a if dt is F32 else a.bitcast(dt)

        this_dst, next_dst, prev_dst, number = (meta(i, I32) for i in range(4))
        same_next, same_prev, spare, step = (meta(4 + i, F32) for i in range(4))
        target = meta(8, I32)
        keep_all = flat[0:MP, meta_at - 9 * MC - MC // 2:meta_at - 9 * MC].bitcast(BF16)
        zero_rows = flat[:, 0:RI * D]

        nt_ps = [psum(f"nt_ps{i}", [P, GROUP * P]) for i in range(2)]
        no_ps = [psum(f"no_ps{i}", [P, GROUP * P]) for i in range(2)]
        et_ps = [psum(f"et_ps{i}", [P, GROUP * P]) for i in range(2)]
        em_ps = psum("em_ps", [P, GROUP * P])
        eb_ps = psum("eb_ps", [P, GROUP * P])
        et_banks, em_banks, eb_banks = [et_ps, et_ps + nt_ps], [[em_ps], [em_ps, no_ps[0]]], [[eb_ps], [eb_ps, no_ps[1]]]
        y_ps = [nt_ps + no_ps, et_ps + [em_ps, eb_ps]]

        zeroed, ident_done, weights_in, src_in = sem("zeroed"), sem("ident_done"), sem("weights_in"), sem("src_in")
        preset, dst_in, meta_step, meta_out = sem("preset"), sem("dst_in"), sem("meta_step"), sem("meta_out")
        numbered, spare_zeroed = sem("numbered"), sem("spare_zeroed")
        block_in, block_turned = sems("block_in"), sems("block_turned")
        nt_full, nt_free, nt_scaled = sems("nt_full", NG - 1), sems("nt_free"), sems("nt_scaled")
        no_full, no_free = sems("no_full"), sems("no_free")
        root_stored = sems("root_stored")
        src_staged, rows_in, edges_turned = sems("src_staged"), sems("rows_in"), sems("edges_turned")
        attr_in, attr_placed = sem("attr_in"), sem("attr_placed")
        et_full, et_free, et_scaled = sems("et_full", NG - 1), [sems("et_free_a"), sems("et_free_b", NG)], sems("et_scaled", NG)
        em_full, em_free = sem("em_full"), sem("em_free")
        keep_in, scan_part, scanned = sem("keep_in"), sem("scan_part"), sem("scanned")
        eb_full, eb_free = sem("eb_full"), sem("eb_free")
        needs_in = sem("needs_in")
        rows_all_in = sem("rows_all_in")
        pool_open, sync_open = sem("pool_open"), sem("sync_open")
        rows_staged = sems("rows_staged")
        staged, scattered = sems("staged"), [sems("scattered_a"), sems("scattered_b")]
        last_root_in, last_x_in, leaky_done = sems("last_root_in", 3), sems("last_x_in", LAST), sem("leaky_done")
        y_full, y_free = sems("y_full", NG), [sems("y_free_a", NG), sems("y_free_b", NG)]
        vec_step, var_done, dev_done = sem("vec_step"), sem("var_done"), sem("dev_done")
        inverted, scaled = sem("inverted"), sem("scaled")
        out_stored = sems("out_stored")

        def blocks(a, width):
            return a[0:NBL * SB, :].rearrange("(b p r) d -> b p (r d)", p=P, r=width)

        def rows_left(a):
            return a[NBL * SB:N, :].rearrange("(p r) d -> p (r d)", r=RI)

        src_full = src[0:NSB * SB].rearrange("(s p r) -> p s r", p=P, r=RI)
        src_left = src[NSB * SB:E].rearrange("(p r) -> p r", r=EJ)
        to_full = rows_to_dram[0:NSB * SB].rearrange("(s p r) -> s p r", p=P, r=RI)
        to_left = rows_to_dram[NSB * SB:E].rearrange("(p r) -> p r", r=EJ)
        attr_full = edge_attr[0:NSB * SB, :].rearrange("(s p r) d -> s p (r d)", p=P, r=RI)
        attr_left = edge_attr[NSB * SB:E, :].rearrange("(p r) d -> p (r d)", r=EJ)
        keep_full = keep_dram[0:NSB * SB].rearrange("(s a e) -> s a e", s=NSB, a=1)
        keep_left = keep_dram[NSB * SB:E].rearrange("(a e) -> a e", a=1)
        dst_row = dst.rearrange("(a e) -> a e", a=1)

        LAYER_ROWS = ((NSB // 2 * RI + EJ) * DMA, NSB // 2 * RI * DMA)

        class Slot:

            def __init__(self, layer, it, odd):
                self.layer, self.it, self.odd, self.full = layer, it, odd, it is not None
                self.s = 2 * it + odd if self.full else NSB
                self.half = it if self.full else NSB // 2
                self.use = layer * SB_USES[odd] + self.half
                self.order = layer * (NSB + 1) + self.s
                self.ep, self.ej = (P, RI) if self.full else (EP, EJ)
                self.egroups = NG if self.full else EG_LEFT
                self.cols = self.ep * self.ej
                self.np = P if self.full else NP
                self.nblocks = 2 if self.full else 1
                self.ngroups = NG * self.nblocks

            def next(self):
                if isinstance(self.s, int) and self.s == NSB - 1:
                    return Slot(self.layer, None, 0)
                return Slot(self.layer, self.it + self.odd, 1 - self.odd)

            def block(self, k):
                return 2 * self.s + k

            def block_use(self, k):
                return self.s

            def ngroup_use(self, j):
                return self.block(j // NG) * (NG // 2) + (j % NG) // 2

            def root_use(self, j):
                return self.block(j // NG)

            def egroup_use(self, q):
                return self.s if self.layer else self.s * (NG // 2) + q // 2

            def bank(self, q):
                return q if self.layer else q % 2

            def freed(self, q):
                return self.egroup(q) - self.layer

            def egroup(self, q):
                return self.layer * EDGE_GROUPS + self.s * NG + q

            def rows(self):
                return self.layer * LAYER_ROWS[self.odd] + (self.half * RI + self.ej) * DMA

            def nodes_turned(self, j):
                if j % NG == NG - 1:
                    return block_turned[j // NG], self.block_use(j // NG) + 1
                return nt_full[j % NG], self.root_use(j) + 1

            def edges_turned(self, q):
                if q == self.egroups - 1:
                    return edges_turned[self.odd], self.use + 1
                return et_full[q], (self.order if q == 0 else self.layer * NSB + self.s) + 1

            def scan_parts(self):
                return self.layer * (NSB * (NG - 1) + EG_LEFT - 1) + self.s * (NG - 1)

        def slots(body, eng, layer):
            for odd in range(2):
                body(Slot(layer, 0, odd))
            with eng.Fori(1, NSB // 2) as it:
                for odd in range(2):
                    body(Slot(layer, it, odd))
            body(Slot(layer, None, 0))

        class Turn:

            def __init__(self, layer, it, odd):
                self.layer, self.odd = layer, odd
                number = 2 * it + odd
                self.first = isinstance(it, int) and number == 0
                self.full = not (isinstance(it, int) and number == 2)
                early = isinstance(it, int) and number <= 2
                self.s = NSB - 2 + number if early else NSB - number
                self.use = layer * SB_USES[odd] + it
                self.ep, self.ej = (P, RI) if self.full else (EP, EJ)
                self.before = it * RI * DMA
                if not odd and not early:
                    self.before = self.before - (RI - EJ) * DMA
                self.held = layer * EDGE_GROUPS + (min((NSB - 1 + number) * NG, EDGE_GROUPS) if early else EDGE_GROUPS)

        def turns(body, eng, layer):
            for number in range(4):
                body(Turn(layer, number // 2, number % 2))
            with eng.Fori(2, NSB // 2) as it:
                for odd in range(2):
                    body(Turn(layer, it, odd))
            body(Turn(layer, NSB // 2, 0))

        def staggered(body, eng, layer):
            body(None, Slot(layer, 0, 0), None)
            body(Slot(layer, 0, 0), Slot(layer, 0, 1), None)
            body(Slot(layer, 0, 1), Slot(layer, 1, 0), Slot(layer, 0, 0))
            with eng.Fori(1, NSB // 2 - 1) as it:
                body(Slot(layer, it, 0), Slot(layer, it, 1), Slot(layer, it - 1, 1))
                body(Slot(layer, it, 1), Slot(layer, it + 1, 0), Slot(layer, it, 0))
            end = NSB // 2 - 1
            body(Slot(layer, end, 0), Slot(layer, end, 1), Slot(layer, end - 1, 1))
            body(Slot(layer, end, 1), Slot(layer, None, 0), Slot(layer, end, 0))
            body(Slot(layer, None, 0), None, Slot(layer, end, 1))
            body(None, None, Slot(layer, None, 0))

        class Middle:

            def __init__(self, it, k):
                it, k = it + k // 2, k % 2
                self.c = 2 * it + k
                self.b = NBL - self.c
                self.it, self.k2 = it, k
                self.use = (NSB + 1 - k) + it
                self.full = not (isinstance(it, int) and self.c == 0)
                self.there = not (isinstance(it, int) and self.c >= BLOCKS)
                self.np = P if self.full else NP
                self.root_use = BLOCKS + self.c

            def ngroup_use(self, g):
                return self.root_use * (NG // 2) + g // 2

            def nodes_turned(self, g):
                if g == NG - 1:
                    return block_turned[self.k2], self.use + 1
                return nt_full[g], self.root_use + 1

        def middle_phase(eng, body):
            body(Middle(0, 0), None)
            body(Middle(0, 1), Middle(0, 0))
            with eng.Fori(1, NSB - 1) as it:
                body(Middle(it, 0), Middle(it - 1, 1))
                body(Middle(it, 1), Middle(it, 0))
            body(Middle(NSB - 1, 0), Middle(NSB - 2, 1))
            body(Middle(NSB - 1, 1), Middle(NSB - 1, 0))
            body(Middle(NSB, 0), Middle(NSB - 1, 1))
            body(None, Middle(NSB, 0))

        def group_at(t, before, g, lag):
            return (t, g - lag) if g >= lag else (before, g - lag + NG)

        def counts(t, n, back):
            groups = t.egroups if t else 0, n.ngroups if n else 0, back.egroups if back else 0
            return *groups, max(groups[0] + 1, groups[1] + 1, (BACK_STEP if t else 0) + groups[2])

        def needed(eng, c):
            return eng.value_load(needs_row[0:1, bass.ds(c, 1)], min_val=1, max_val=LAYER_ROWS[1])

        def wait_scatters(eng, layer, need):
            eng.wait_ge(scattered[layer][0], need + EJ * DMA)
            eng.wait_ge(scattered[layer][1], need)

        class Last:

            def __init__(self, it, k):
                it, k = it + k // LAST, k % LAST
                self.c = LAST * it + k
                self.b = NBL - self.c
                self.use2, self.use3 = it * (LAST // 2) + k // 2, it * (LAST // 3) + k // 3
                self.it, self.k, self.k2, self.k3 = it, k, k % 2, k % 3
                self.full = not (isinstance(self.c, int) and self.c == 0)
                self.n = P if self.full else NP
                self.there = not (isinstance(self.c, int) and self.c >= BLOCKS)

        def last_phase(eng, body):
            for k in range(LAST):
                body(0, k)
            with eng.Fori(1, NBL // LAST - 1) as it:
                for k in range(LAST):
                    body(it, k)
            for k in range(LAST + 1):
                body(NBL // LAST - 1, k)

        block = ctx.enter_context(nc.Block())

        @block.sync
        def _(sp):
            sp.dma_start(src_all[:, 0:NSB * RI].rearrange("p (s r) -> p s r", r=RI), src_full).then_inc(src_in, DMA)
            sp.wait_ge(preset, 1)
            sp.dma_start(src_all[0:EP, NSB * RI:NSB * RI + EJ], src_left).then_inc(src_in, DMA)
            for layer in range(2):
                w_msg, w_e, w_r, bias = weights[4 * layer:4 * layer + 4]
                sp.dma_start(w_edge[0:D, layer, :], w_msg).then_inc(weights_in, DMA)
                sp.dma_start(w_edge[D:K, layer, :], w_e).then_inc(weights_in, DMA)
                sp.dma_start(w_root[0:D, layer, :], w_r).then_inc(weights_in, DMA)
                sp.dma_start(w_root[D:D + 1, layer, :], bias.rearrange("(a d) -> a d", a=1)).then_inc(weights_in, DMA)
            def store_metadata():
                sp.wait_ge(zeroed, 1)
                for layer in range(2):
                    for i in range(SPARE // SB):
                        to = root[layer][N + i * SB:N + (i + 1) * SB, :].rearrange("(p r) d -> p (r d)", r=RI)
                        sp.dma_start(to, zero_rows).then_inc(spare_zeroed, DMA)
                sp.wait_ge(meta_step, META_STEPS)
                sp.dma_start(rows_to_dram.rearrange("(p c) -> p c", c=MC), target).then_inc(meta_out, DMA)
                sp.dma_start(keep_dram.rearrange("(p c) -> p c", c=MC), keep_all).then_inc(meta_out, DMA)
                sp.dma_start(needs_dram, needs[0:NEEDS, :]).then_inc(meta_out, DMA)

                sp.wait_ge(meta_out, 3 * DMA)
                to_rows = rows_to_dram[0:NSB * SB].rearrange("(s p r) -> p s r", p=P, r=RI)
                sp.dma_start(rows_all[:, 0:NSB * RI].rearrange("p (s r) -> p s r", r=RI), to_rows).then_inc(rows_all_in, DMA)
                sp.dma_start(rows_all[0:EP, NSB * RI:NSB * RI + EJ], to_left).then_inc(rows_all_in, DMA)
                sp.dma_start(needs_row[:], needs_dram.rearrange("b a -> a b")).then_inc(needs_in, DMA)

            def load_attr(t):
                sp.wait_ge(attr_placed, t.order)
                if t.full:
                    sp.dma_start(attr[:], attr_full[t.s]).then_inc(attr_in, DMA)
                else:
                    sp.dma_start(attr[0:EP, 0:EJ * DE], attr_left).then_inc(attr_in, DMA)

            def loads(t):
                for k in range(0 if t.layer else t.nblocks):
                    sp.wait_ge(block_turned[k], t.block_use(k))
                    if t.full:
                        sp.dma_start(nodes_in[:, k, :], blocks(x, RI)[t.block(k)]).then_inc(block_in[k], DMA)
                    else:
                        sp.dma_start(nodes_in[0:NP, k, :], rows_left(x)).then_inc(block_in[k], DMA)
                    if k == 0:
                        load_attr(t)
                if t.layer:
                    load_attr(t)
                elif isinstance(t.s, int) and t.s == 0:
                    store_metadata()

            def stage(t):
                if t.first:
                    sp.wait_ge(block_turned[0], NSB + 1)
                    sp.wait_ge(block_turned[1], NSB)
                sp.wait_ge(scattered[t.layer][t.odd], t.before)
                sp.wait_ge(eb_free, t.held)
                sp.sem_inc(sync_open, 1)
                of = hold[0:t.ep, bass.ds(t.s * RI, t.ej), :].rearrange("p r d -> p (r d)")
                sp.dma_start(nodes_in[0:t.ep, t.odd, 0:t.ej * D], of).then_inc(staged[t.odd], DMA)
                if t.full:
                    sp.dma_start(rows_now[:, t.odd, :], to_full[t.s]).then_inc(rows_staged[t.odd], DMA)
                else:
                    sp.dma_start(rows_now[0:EP, t.odd, 0:EJ], to_left).then_inc(rows_staged[t.odd], DMA)

            slots(loads, sp, 0)
            turns(stage, sp, 0)
            slots(loads, sp, 1)
            sp.wait_ge(eb_full, 2 * EDGE_GROUPS)
            sp.wait_ge(needs_in, DMA)

            def load_x(t):
                x_at = blocks(x, RI)[t.b] if t.full else rows_left(x)
                sp.dma_start(last_x[t.k][0:t.n, :], x_at).then_inc(last_x_in[t.k], DMA)

            def load(it, k):
                t, ahead = Last(it, k), Last(it, k + 3)
                need = needed(sp, t.c)
                if not (isinstance(t.c, int) and t.c < 3):
                    sp.wait_ge(y_full[NG - 1], t.c - 2)
                    sp.sem_inc(sync_open, 1)
                    if ahead.there:
                        load_x(ahead)
                wait_scatters(sp, 1, need)
                sp.sem_inc(sync_open, 1)
                root_at = blocks(root[1], RI)[t.b] if t.full else rows_left(root[1])
                sp.dma_start(last_root[t.k3][0:t.n, :], root_at).then_inc(last_root_in[t.k3], DMA)

            for k in range(LAST):
                if k == LAST - 1:
                    sp.wait_ge(scattered[1][0], RI * DMA)
                load_x(Last(0, k))
            last_phase(sp, load)

        @block.gpsimd
        def _(pool):
            nc.gpsimd.memset(ident[:], 0.0).then_inc(numbered, 1)
            pool.wait_ge(numbered, 1)
            nc.gpsimd.affine_select(out=ident[:], in_=ident[:], compare_op=ALU.not_equal, fill=1.0, base=0,
                                    pattern=[[-1, P]], channel_multiplier=1).then_inc(ident_done, 1)
            nc.gpsimd.iota(number, pattern=[[1, MC]], base=0, channel_multiplier=MC).then_inc(numbered, 1)
            nc.gpsimd.iota(bound_i[:], pattern=[[0, 1]], base=NBL * SB, channel_multiplier=-SB).then_inc(numbered, 1)

            def gather(t):
                pool.wait_ge(src_staged[t.odd], t.layer * SB_USES[0] + t.half + 1)
                pool.wait_ge(edges_turned[t.odd], t.use)
                pool.sem_inc(pool_open, 1)
                for i in range(t.ej):
                    nc.gpsimd.indirect_dma_start(
                        out=gathered[t.odd][0:t.ep, i, 0:D], out_offset=None, in_=(x, root[0])[t.layer],
                        in_offset=bass.IndirectOffsetOnAxis(ap=src_now[0:t.ep, t.odd, i:i + 1], axis=0),
                    ).then_inc(rows_in[t.odd], DMA)

            def scatter(t):
                pool.wait_ge(staged[t.odd], DMA * (t.use + 1))
                pool.wait_ge(rows_staged[t.odd], DMA * (t.use + 1))
                pool.sem_inc(pool_open, 1)
                for i in range(t.ej):
                    nc.gpsimd.indirect_dma_start(
                        out=root[t.layer],
                        out_offset=bass.IndirectOffsetOnAxis(ap=rows_now[0:t.ep, t.odd, i:i + 1], axis=0),
                        in_=nodes_in[0:t.ep, t.odd, i * D:(i + 1) * D], in_offset=None, compute_op=ALU.add,
                    ).then_inc(scattered[t.layer][t.odd], DMA)

            def scatter_held(t):
                pool.wait_ge(eb_free, t.held)
                if t.before:
                    pool.wait_ge(scattered[1][t.odd], t.before)
                for i in range(t.s * RI, t.s * RI + t.ej):
                    nc.gpsimd.indirect_dma_start(
                        out=root[1], out_offset=bass.IndirectOffsetOnAxis(ap=rows_all[0:t.ep, i:i + 1], axis=0),
                        in_=hold[0:t.ep, i, :], in_offset=None, compute_op=ALU.add,
                    ).then_inc(scattered[1][t.odd], DMA)

            for layer in range(2):
                slots(gather, pool, layer)
                pool.wait_ge(spare_zeroed, 2 * (SPARE // SB) * DMA)
                for half in range(2):
                    pool.wait_ge(root_stored[half], (layer + 1) * BLOCKS * DMA)
                if layer == 0:
                    turns(scatter, pool, layer)
                else:
                    pool.wait_ge(rows_all_in, 2 * DMA)
                    for n in range(NSB + 1):
                        scatter_held(Turn(1, n // 2, n % 2))
                for odd in range(2):
                    pool.wait_ge(scattered[layer][odd], LAYER_ROWS[odd])

        @block.tensor
        def _(pe):
            pe.wait_ge(ident_done, 1)
            pe.wait_ge(weights_in, 8 * DMA)
            pe.wait_ge(zeroed, 2)

            def turn_nodes(t, j):
                k, g, bank = j // NG, j % NG, j % 2
                if g == 0:
                    pe.wait_ge(block_in[k], DMA * (t.block_use(k) + 1))
                pe.wait_ge(nt_free[bank], t.ngroup_use(j))
                for i in range(GROUP):
                    at = (g * GROUP + i) * D
                    last = nc.tensor.transpose(nt_ps[bank][0:D, i * t.np:(i + 1) * t.np],
                                               nodes_in[0:t.np, k, at:at + D], ident[0:t.np, 0:t.np])
                last.then_inc(t.nodes_turned(j)[0], 1)

            def root_of(t, j):
                bank = j % 2
                pe.wait_ge(nt_free[bank], t.ngroup_use(j) + 1)
                pe.wait_ge(no_free[bank], t.ngroup_use(j))
                for i in range(GROUP):
                    last = nc.tensor.matmul(no_ps[bank][0:t.np, i * D:(i + 1) * D],
                                            nodes_t[0:D + 1, bank, i * t.np:(i + 1) * t.np],
                                            w_root[0:D + 1, t.layer, :], start=True, stop=True)
                last.then_inc(no_full[bank], 1)

            def turn_edges(t, q):
                bank = t.bank(q)
                if q == 0:
                    pe.wait_ge(rows_in[t.odd], t.rows())
                    pe.wait_ge(attr_placed, t.order + 1)
                pe.wait_ge(et_free[t.layer][bank], t.egroup_use(q))
                for i in range(GROUP):
                    last = nc.tensor.transpose(et_banks[t.layer][bank][:, i * t.ep:(i + 1) * t.ep],
                                               gathered[t.odd][0:t.ep, q * GROUP + i, :], ident[0:t.ep, 0:t.ep])
                last.then_inc(t.edges_turned(q)[0], 1)

            def messages(t, q):
                pe.wait_ge(et_free[t.layer][t.bank(q)], t.egroup_use(q) + 1)
                pe.wait_ge(em_free, t.freed(q))
                em, turned = (of[t.layer][q % (1 + t.layer)] for of in (em_banks, edges_t_of))
                ins = nc.tensor.matmul(em[0:D, 0:GROUP * t.ep], w_edge[:, t.layer, :],
                                       turned[:, 0:GROUP * t.ep], start=True, stop=True)
                ins.then_inc(em_full, 1)

            def turn_back(t, q):
                pe.wait_ge(scanned, t.order + 1)
                pe.wait_ge(eb_free, t.freed(q))
                eb = eb_banks[t.layer][q % (1 + t.layer)]
                for i in range(GROUP):
                    cols = msgs[t.odd][0:D, q * GROUP + i:t.cols:t.ej]
                    last = nc.tensor.transpose(eb[0:t.ep, i * D:(i + 1) * D], cols, ident[0:D, 0:D])
                last.then_inc(eb_full, 1)

            def slot(t, n, back):
                egroups, ngroups, bgroups, steps = counts(t, n, back)
                first_back = BACK_STEP if t else 0
                for j in range(steps):
                    if j < egroups:
                        turn_edges(t, j)
                    if j < ngroups:
                        turn_nodes(n, j)
                    if 1 <= j <= egroups:
                        messages(t, j - 1)
                    if 1 <= j <= ngroups:
                        root_of(n, j - 1)
                    if 0 <= j - first_back < bgroups:
                        turn_back(back, j - first_back)

            def middle(t, before):
                for g in range(NG if t else 2):
                    if t:
                        if g == 0:
                            pe.wait_ge(block_in[t.k2], DMA * (t.use + 1))
                        pe.wait_ge(nt_free[g % 2], t.ngroup_use(g))
                        for i in range(GROUP):
                            at = (g * GROUP + i) * D
                            last = nc.tensor.transpose(nt_ps[g % 2][0:D, i * t.np:(i + 1) * t.np],
                                                       middle_in[t.k2][0:t.np, at:at + D], ident[0:t.np, 0:t.np])
                        last.then_inc(t.nodes_turned(g)[0], 1)
                    of, h = group_at(t, before, g, 2)
                    if of:
                        pe.wait_ge(nt_free[h % 2], of.ngroup_use(h) + 1)
                        pe.wait_ge(no_free[h % 2], of.ngroup_use(h))
                        for i in range(GROUP):
                            last = nc.tensor.matmul(no_ps[h % 2][0:of.np, i * D:(i + 1) * D],
                                                    nodes_t[0:D + 1, h % 2, i * of.np:(i + 1) * of.np],
                                                    w_root[0:D + 1, 1, :], start=True, stop=True)
                        last.then_inc(no_full[h % 2], 1)

            def edges(t):
                for q in range(t.egroups):
                    turn_edges(t, q)
                for q in range(t.egroups):
                    messages(t, q)
                for q in range(t.egroups):
                    turn_back(t, q)

            staggered(slot, pe, 0)
            middle_phase(pe, middle)
            for bank in range(2):
                pe.wait_ge(nt_free[bank], 2 * BLOCKS * (NG // 2))
                pe.wait_ge(no_free[bank], 2 * BLOCKS * (NG // 2))
            slots(edges, pe, 1)

            pe.wait_ge(eb_free, 2 * EDGE_GROUPS)

            def add(it, k):
                t = Last(it, k)
                pe.wait_ge(last_x_in[t.k], DMA * (t.it + 1))
                pe.wait_ge(leaky_done, t.c + 1)
                for g in range(NG):
                    pe.wait_ge(y_free[t.k2][g], t.use2)
                    cols = slice(g * GROUP * D, (g + 1) * GROUP * D)
                    y = y_ps[t.k2][g][0:t.n, 0:GROUP * D]
                    nc.tensor.matmul(y, ident[0:t.n, 0:t.n], last_x[t.k][0:t.n, cols], start=True, stop=False)
                    nc.tensor.matmul(y, ident[0:t.n, 0:t.n], last_root[t.k3][0:t.n, cols], start=False,
                                     stop=True).then_inc(y_full[g], 1)

            last_phase(pe, add)

        @block.scalar
        def _(act):
            act.dma_start(this_dst, dst.rearrange("(p c) -> p c", c=MC)).then_inc(dst_in, DMA)
            act.wait_ge(preset, 3)
            last = (MP - 1) * MC
            act.dma_start(next_dst[0:MP - 1, :], dst[1:last + 1].rearrange("(p c) -> p c", c=MC)).then_inc(dst_in, DMA)
            act.dma_start(next_dst[MP - 1:MP, 0:MC - 1], dst_row[:, last + 1:E]).then_inc(dst_in, DMA)
            act.dma_start(prev_dst[0:1, 1:MC], dst_row[:, 0:MC - 1]).then_inc(dst_in, DMA)
            act.dma_start(prev_dst[1:MP, :], dst[MC - 1:E - 1].rearrange("(p c) -> p c", c=MC)).then_inc(dst_in, DMA)
            with nc.allow_non_contiguous_dma(reason="the last dst of each superblock"):
                act.dma_start(ends[0:NEEDS, 0:NSB],
                              dst_row[:, SB - 1:E:SB].to_broadcast([NEEDS, NSB])).then_inc(dst_in, DMA)

            def read_nodes(t, j):
                bank = j % 2
                act.wait_ge(*t.nodes_turned(j))
                act.wait_ge(no_full[bank], t.ngroup_use(j))
                cols = slice(0, GROUP * t.np)
                nc.scalar.activation(nodes_t[0:D, bank, cols], nt_ps[bank][0:D, cols], ACT.Copy).then_inc(nt_free[bank], 1)

            def read_edges(t, q):
                bank, turned = t.bank(q), edges_t_of[t.layer][q % (1 + t.layer)]
                act.wait_ge(*t.edges_turned(q))
                act.wait_ge(em_full, t.freed(q))
                cols = slice(0, GROUP * t.ep)
                nc.scalar.activation(turned[:, cols], et_banks[t.layer][bank][:, cols], ACT.Copy,
                                     scale=slopes[:, 0:1] if t.layer else 1.0,
                                     ).then_inc((et_scaled if t.layer else et_free[0])[bank], 1)

            def read_messages(t, q):
                act.wait_ge(em_full, t.egroup(q) + 1)
                if q == 0:
                    act.wait_ge(scanned, t.order)
                    if t.layer == 0 and isinstance(t.s, int) and t.s == 0:
                        act.wait_ge(meta_out, 3 * DMA)
                    view = keep_full[t.s] if t.full else keep_left
                    act.dma_start(keep[0:D, 0:t.cols], view.to_broadcast([D, t.cols])).then_inc(keep_in, DMA)
                to = msgs[t.odd][0:D, 0:t.cols].rearrange("d (p r) -> d p r", r=t.ej)[:, :, q * GROUP:(q + 1) * GROUP]
                em = em_banks[t.layer][q % (1 + t.layer)]
                nc.scalar.activation(to, em[0:D, 0:GROUP * t.ep].rearrange("d (i p) -> d p i", i=GROUP),
                                     ACT.Copy).then_inc(em_free, 1)

            def store_half(layer, t, half, b):
                to = blocks(root[layer], RI)[b] if t.full else rows_left(root[layer])
                at = slice(half * HALF * D, (half + 1) * HALF * D)
                act.dma_start(to[:, at], root_out[0:t.np, half, :]).then_inc(root_stored[half], DMA)

            def store_root(t, j):
                act.wait_ge(no_free[0], t.ngroup_use(j - 1) + 1)
                act.wait_ge(no_free[1], t.ngroup_use(j) + 1)
                store_half(0, t, (j % NG) // 2, t.block(j // NG))

            def slot(t, n, back):
                egroups, ngroups, bgroups, steps = counts(t, n, back)
                for j in range(steps):
                    if j < egroups:
                        read_edges(t, j)
                    if j < ngroups:
                        read_nodes(n, j)
                    if 1 <= j <= egroups:
                        read_messages(t, j - 1)
                    if 3 <= j <= ngroups and j % 2:
                        store_root(n, j - 2)
                    if t and t.full and t.layer == 0 and j == 1:
                        store_root(t, t.ngroups - 1)
                if n and not n.full:
                    store_root(n, ngroups - 1)

            def load_middle(t):
                if t.k2 == 0:
                    need = needed(act, t.c + 1)
                    act.wait_ge(block_turned[0], t.use)
                    wait_scatters(act, 0, need)
                else:
                    act.wait_ge(block_turned[1], t.use)
                of = blocks(root[0], RI)[t.b] if t.full else rows_left(root[0])
                act.dma_start(middle_in[t.k2][0:t.np, :], of).then_inc(block_in[t.k2], DMA)

            def middle(t, before):
                for g in range(NG if t else 2):
                    if t:
                        act.wait_ge(*t.nodes_turned(g))
                        act.wait_ge(no_full[g % 2], t.ngroup_use(g))
                        cols = slice(0, GROUP * t.np)
                        nc.scalar.activation(nodes_t[0:D, g % 2, cols], nt_ps[g % 2][0:D, cols], ACT.Copy,
                                             scale=SLOPE).then_inc(nt_scaled[g % 2], 1)
                    of, h = group_at(t, before, g, 2)
                    if of:
                        bank, half = h % 2, h // 2
                        act.wait_ge(no_full[bank], of.ngroup_use(h) + 1)
                        if bank == 0:
                            act.wait_ge(root_stored[half], DMA * of.root_use)
                        at = slice(bank * GROUP * D, (bank + 1) * GROUP * D)
                        nc.scalar.copy(root_out[0:of.np, half, at], no_ps[bank][0:of.np, 0:GROUP * D],
                                       ).then_inc(no_free[bank], 1)
                        if bank == 1:
                            act.wait_ge(no_free[1], of.ngroup_use(h) + 1)
                            store_half(1, of, half, of.b)
                if t:
                    ahead = Middle(t.it, t.k2 + 2)
                    if ahead.there:
                        load_middle(ahead)

            staggered(slot, act, 0)
            act.wait_ge(needs_in, DMA)
            for k in range(2):
                load_middle(Middle(0, k))
            middle_phase(act, middle)

            def edges(t):
                for q in range(t.egroups + 1):
                    if q < t.egroups:
                        read_edges(t, q)
                    if q:
                        read_messages(t, q - 1)

            slots(edges, act, 1)

            def deviation(t):
                act.wait_ge(var_done, t.c + 1)
                nc.scalar.activation(small[0:t.n, t.k2, 3, :], small[0:t.n, t.k2, 2, :], ACT.Sqrt,
                                     bias=eps[0:t.n, 0:1]).then_inc(dev_done, 1)

            def normalise(t, g):
                for i in range(GROUP):
                    r = g * GROUP + i
                    last = nc.scalar.activation(
                        last_out[t.k2][0:t.n, r * D:(r + 1) * D], y_ps[t.k2][g][0:t.n, i * D:(i + 1) * D],
                        ACT.Identity, bias=small[0:t.n, t.k2, 5, r:r + 1], scale=small[0:t.n, t.k2, 4, r:r + 1])
                last.then_inc(y_free[t.k2][g], 1)

            def finish(it, k):
                t, following = Last(it, k), Last(it, k + 1)
                act.wait_ge(scaled, t.c + 1)
                act.wait_ge(out_stored[t.k2], DMA * t.use2)
                for g in range(NG):
                    if g == NG - 1 and following.there:
                        deviation(following)
                    normalise(t, g)
                act.wait_ge(y_free[t.k2][NG - 1], t.use2 + 1)
                out_at = blocks(out, RI)[t.b] if t.full else rows_left(out)
                act.dma_start(out_at, last_out[t.k2][0:t.n, :]).then_inc(out_stored[t.k2], DMA)

            deviation(Last(0, 0))
            last_phase(act, finish)
            for k2 in range(2):
                act.wait_ge(out_stored[k2], DMA * ((BLOCKS + 1 - k2) // 2))

        @block.vector
        def _(dve):
            nc.vector.memset(src_all[:, NSB * RI:], 0).then_inc(preset, 1)
            nc.vector.memset(next_dst, -1).then_inc(preset, 1)
            nc.vector.memset(prev_dst, -1).then_inc(preset, 1)
            nc.vector.memset(zero_rows, 0.0).then_inc(zeroed, 1)
            nc.vector.memset(nodes_t[D:D + 1, :, :], 1.0)
            nc.vector.memset(eps[:], EPS)
            nc.vector.memset(slopes[0:D, :], SLOPE)
            nc.vector.memset(slopes[D:K, :], 1.0)
            nc.vector.memset(msgs[1][0:D, SB - 1:SB], -BIG).then_inc(zeroed, 1)

            def stage_src(s, odd, before):
                dve.wait_ge(rows_in[odd], before)
                nc.vector.tensor_copy(src_now[:, odd, :], src_all[:, bass.ds(s * RI, RI)]).then_inc(src_staged[odd], 1)

            def link(ins):
                link.n += 1
                ins.then_inc(meta_step, 1)
                dve.wait_ge(meta_step, link.n)
            link.n = 0

            def metadata():
                dve.wait_ge(dst_in, 6 * DMA)
                dve.wait_ge(numbered, 3)
                link(nc.vector.tensor_tensor(same_next, this_dst, next_dst, ALU.is_equal))
                link(nc.vector.tensor_scalar(number, number, SPARE - 1, None, ALU.bitwise_and))
                link(nc.vector.tensor_scalar(spare, number, float(N), None, ALU.add))
                link(nc.vector.tensor_tensor(step, spare, this_dst, ALU.subtract))
                link(nc.vector.tensor_tensor(step, step, same_next, ALU.mult))
                link(nc.vector.tensor_tensor(target, step, this_dst, ALU.add))
                link(nc.vector.tensor_tensor(same_prev, this_dst, prev_dst, ALU.is_equal))
                link(nc.vector.tensor_scalar(same_prev, same_prev, -0.5, 2.0, ALU.add, ALU.mult))
                link(nc.vector.tensor_scalar(keep_all, same_prev, BIG, None, ALU.mult))
                link(nc.vector.memset(ends[:, NSB - 1:], N))
                link(nc.vector.tensor_copy(bound[:], bound_i[:]))
                link(nc.vector.memset(share[:], 0.0))
                link(nc.vector.memset(share[:, 1:NSB:2], float(RI * DMA)))
                link(nc.vector.tensor_scalar(reach[0:NEEDS, :], ends[0:NEEDS, :], bound[0:NEEDS, 0:1], None, ALU.is_ge))
                link(nc.vector.tensor_tensor(reach[0:NEEDS, :], reach[0:NEEDS, :], share[0:NEEDS, :], ALU.mult))
                link(nc.vector.tensor_reduce(needs_f[0:NEEDS, :], reach[0:NEEDS, :], AX_X, ALU.add))
                link(nc.vector.tensor_copy(needs[0:NEEDS, :], needs_f[0:NEEDS, :]))
                assert link.n == META_STEPS

            def place_attr(t):
                dve.wait_ge(attr_in, DMA * (t.order + 1))
                dve.wait_ge(edges_turned[t.odd], t.use)
                nc.vector.tensor_copy(gathered[t.odd][0:t.ep, 0:t.ej, D:K],
                                      attr[0:t.ep, 0:t.ej * DE].rearrange("p (r k) -> p r k", k=DE),
                                      ).then_inc(attr_placed, 1)

            def leaky_edges(t, q):
                cols, turned = slice(0, GROUP * t.ep), edges_t_of[1][q % 2]
                dve.wait_ge(et_scaled[q], t.egroup_use(q) + 1)
                nc.vector.tensor_tensor(turned[:, cols], et_banks[1][q][:, cols], turned[:, cols],
                                        ALU.max).then_inc(et_free[1][q], 1)

            def read_root(t, j):
                bank, half = j % 2, (j % NG) // 2
                dve.wait_ge(no_full[bank], t.ngroup_use(j) + 1)
                if j % 2 == 0:
                    dve.wait_ge(root_stored[half], DMA * t.root_use(j))
                at = slice((j % 2) * GROUP * D, (j % 2 + 1) * GROUP * D)
                nc.vector.tensor_copy(root_out[0:t.np, half, at], no_ps[bank][0:t.np, 0:GROUP * D]).then_inc(no_free[bank], 1)

            def scan(t, c):
                if c == 0:
                    dve.wait_ge(scanned, t.order)
                    dve.wait_ge(em_free, t.egroup(t.egroups))
                    dve.wait_ge(keep_in, DMA * (t.order + 1))
                    start = msgs[1 - t.odd][0:D, SB - 1:SB]
                else:
                    start = msgs[t.odd][0:D, c * SCAN - 1:c * SCAN]
                    dve.wait_ge(scan_part, t.scan_parts() + c)
                at = slice(c * SCAN, min((c + 1) * SCAN, t.cols))
                ins = nc.vector.tensor_tensor_scan(msgs[t.odd][0:D, at], keep[0:D, at], msgs[t.odd][0:D, at],
                                                   start, ALU.min, ALU.max)
                ins.then_inc(scanned if at.stop == t.cols else scan_part, 1)

            def read_back(t, q):
                if q == 0 and t.layer == 0 and isinstance(t.s, int) and t.s == 0:
                    dve.wait_ge(meta_out, 3 * DMA)
                    dve.wait_ge(spare_zeroed, 2 * (SPARE // SB) * DMA)
                dve.wait_ge(eb_full, t.egroup(q) + 1)
                if t.full:
                    to = hold[:, bass.ds(t.s * RI + q * GROUP, GROUP), :]
                else:
                    to = hold[0:EP, NSB * RI + q * GROUP:NSB * RI + (q + 1) * GROUP, :]
                eb = eb_banks[t.layer][q % (1 + t.layer)]
                nc.vector.tensor_copy(to, eb[0:t.ep, 0:GROUP * D].rearrange("p (r d) -> p r d", d=D)).then_inc(eb_free, 1)

            def slot(t, n, back):
                egroups, ngroups, bgroups, steps = counts(t, n, back)
                first_back = BACK_STEP if t else 0
                scans = -(-t.cols // SCAN) if t else 0
                if not t and not back:
                    place_attr(n)
                for j in range(max(steps, egroups + 1 + scans)):
                    if 1 <= j <= ngroups:
                        read_root(n, j - 1)
                    if t and t.full and j == 2:
                        place_attr(t.next())
                    if j == 0 and t and t.full:
                        stage_src(t.s + 2, t.odd, t.rows())
                    if 0 <= j - first_back < bgroups:
                        read_back(back, j - first_back)
                    if 0 <= j - egroups - 1 < scans:
                        scan(t, j - egroups - 1)

            def edges(t):
                if t.full:
                    stage_src(t.s + 2, t.odd, t.rows())
                for q in range(t.egroups):
                    leaky_edges(t, q)
                if t.full:
                    place_attr(t.next())
                for c in range(-(-t.cols // SCAN)):
                    scan(t, c)
                for q in range(t.egroups):
                    read_back(t, q)

            def leaky_nodes(t, before):
                for g in range(NG if t else 0):
                    cols = slice(0, GROUP * t.np)
                    dve.wait_ge(nt_scaled[g % 2], t.ngroup_use(g) - BLOCKS * (NG // 2) + 1)
                    nc.vector.tensor_tensor(nodes_t[0:D, g % 2, cols], nt_ps[g % 2][0:D, cols],
                                            nodes_t[0:D, g % 2, cols], ALU.max).then_inc(nt_free[g % 2], 1)

            dve.wait_ge(src_in, 2 * DMA)
            for layer in range(2):
                if layer == 0:
                    stage_src(0, 0, 0)
                    stage_src(1, 1, 0)
                    metadata()
                    staggered(slot, dve, 0)
                else:
                    stage_src(0, 0, LAYER_ROWS[0])
                    stage_src(1, 1, LAYER_ROWS[1])
                    middle_phase(dve, leaky_nodes)
                    place_attr(Slot(1, 0, 0))
                    slots(edges, dve, 1)

            def leaky(t):
                dve.wait_ge(last_root_in[t.k3], DMA * (t.use3 + 1))
                r = last_root[t.k3][0:t.n, :]
                nc.vector.scalar_tensor_tensor(r, r, SLOPE, r, ALU.mult, ALU.max).then_inc(leaky_done, 1)

            def moments(it, k):
                t, ahead = Last(it, k), Last(it, k + 2)
                mean, diff, var, dev, inv, shift = (small[0:t.n, t.k2, i, :] for i in range(6))

                def step_done(ins, i):
                    ins.then_inc(vec_step, 1)
                    dve.wait_ge(vec_step, t.c * NORM_STEPS + i + 1)

                for g in range(NG):
                    dve.wait_ge(y_full[g], t.c + 1)
                    for i in range(GROUP):
                        last = nc.vector.bn_stats(stats[0:t.n, g * GROUP + i, :],
                                                  y_ps[t.k2][g][0:t.n, i * D:(i + 1) * D])
                step_done(last, 0)
                even, odd = stats[0:t.n, :, 1], stats[0:t.n, :, 4]
                if not (isinstance(t.c, int) and t.c < 2):
                    dve.wait_ge(y_free[t.k2][NG - 1], t.use2)
                nc.vector.tensor_tensor(diff, even, odd, ALU.subtract)
                nc.vector.tensor_tensor(mean, even, odd, ALU.add)
                step_done(nc.vector.tensor_tensor(var, stats[0:t.n, :, 2], stats[0:t.n, :, 5], ALU.add), 1)
                step_done(nc.vector.scalar_tensor_tensor(diff, diff, 0.25, diff, ALU.mult, ALU.mult), 2)
                nc.vector.scalar_tensor_tensor(var, var, 1.0 / D, diff, ALU.mult, ALU.add).then_inc(var_done, 1)
                dve.wait_ge(dev_done, t.c + 1)
                nc.vector.reciprocal(inv, dev).then_inc(inverted, 1)
                dve.wait_ge(inverted, t.c + 1)
                nc.vector.scalar_tensor_tensor(shift, mean, -0.5, inv, ALU.mult, ALU.mult).then_inc(scaled, 1)
                if ahead.there:
                    leaky(ahead)

            dve.wait_ge(eb_free, 2 * EDGE_GROUPS)
            leaky(Last(0, 0))
            leaky(Last(0, 1))
            last_phase(dve, moments)


_WEIGHTS = [f"L0_gnn_{w}" for w in ("W1_msg", "W1_edge", "W1_root", "b1", "W2_msg", "W2_edge", "W2_root", "b2")]
_INS = ["x", "src", "dst", "edge_attr_32"] + _WEIGHTS


def kernel(**inputs):
    import numpy as _np
    import concourse.bacc as _bacc
    from concourse import mybir as _mybir
    from concourse.bass_utils import run_bass_kernel_spmd as _run

    nc = _bacc.Bacc("TRN2", target_bir_lowering=False, num_devices=1, dynamic_dma_scratch_size=8192)
    arrays, args = {}, []
    for name in _INS:
        a = _np.ascontiguousarray(inputs[name])
        arrays[f"in_{name}_dram"] = a
        args.append(nc.dram_tensor(f"in_{name}_dram", a.shape, _mybir.dt.from_np(a.dtype), kind="ExternalInput").ap())
    shape = inputs["x"].shape
    out = nc.dram_tensor("out_0_dram", tuple(shape), _mybir.dt.float32, kind="ExternalOutput").ap()
    gnn(nc, *args[:4], args[4:], out)
    r = _run(nc, [arrays], core_ids=[0])
    return r.results[0]["out_0_dram"]
```
